# Optimizing a Trainium2 kernel written in Bass

```python
import numpy as np
import jax
import jax.numpy as jnp

def _softmax(x, axis=-1):
    return jax.nn.softmax(x, axis=axis)

def _gelu(x):
    return jax.nn.gelu(x, approximate=True)

def _silu(x):
    return jax.nn.silu(x)

def _sigmoid(x):
    return jax.nn.sigmoid(x)

def _layernorm(x, axis=-1, eps=1e-05):
    m = jnp.mean(x, axis=axis, keepdims=True)
    v = jnp.var(x, axis=axis, keepdims=True)
    return (x - m) / jnp.sqrt(v + eps)

def _scatter_add(tgt, idx, src, axis=0):
    return tgt.at[idx].add(src)

def _segment_sum(src, seg, n):
    return jax.ops.segment_sum(src, seg, n)
kernel_name = 'mk_gnn_ffn_d1_gnn_r8_44c12b'

def setup_inputs(seed: int=0):
    np.random.seed(seed)
    _w = jnp.asarray

    def _rec_inputs():
        import jax
        import jax.numpy as jnp
        _gk = jax.random.key(seed)
        x = -0.0003713 + 1 * jax.random.normal(jax.random.fold_in(_gk, 1), (6250, 256), jnp.float32)
        _s = jax.random.randint(jax.random.fold_in(_gk, 2), (50000,), 0, 6250, jnp.int32)
        _d = jax.random.randint(jax.random.fold_in(_gk, 3), (50000,), 0, 6250, jnp.int32)
        _loop = jnp.arange(6250, dtype=jnp.int32)
        src = jnp.concatenate([_s, _d, _loop])
        dst = jnp.concatenate([_d, _s, _loop])
        _o = jnp.argsort(dst, stable=True)
        src = src[_o]
        dst = dst[_o]
        edge_type_400 = jax.random.randint(jax.random.fold_in(_gk, 12), (106250,), 0, 400, jnp.int32)
        return (x, src, dst, edge_type_400)
    x, src, dst, edge_type_400 = _rec_inputs()

    def _L0_gnn_setup():
        import jax, jax.numpy as jnp
        import numpy as np
        N = 6250
        D = 256
        E = 40000
        R = 400

        def _mgcn_conv(x, edge_index, edge_type, rel, W_in, W_out, W_loop, b, n):
            src, dst = (edge_index[0], edge_index[1])
            e = edge_index.shape[1]
            half = e // 2
            m = x[src] * rel[edge_type]
            m = jnp.concatenate([m[:half] @ W_in, m[half:] @ W_out], 0)
            deg = jax.ops.segment_sum(jnp.ones((e,), x.dtype), dst, num_segments=n)
            norm = 1.0 / jnp.maximum(deg, 1.0)
            agg = jax.ops.segment_sum(m * norm[dst][:, None], dst, num_segments=n)
            return jnp.tanh(agg + x @ W_loop + b)
        key = jax.random.key(seed)
        ks = jax.random.split(key, 12)
        s = 0.05
        w = lambda k, shp: jax.random.normal(k, shp, jnp.float32) * s
        return {'emb': jax.random.normal(ks[0], (N, D), jnp.float32), 'edge_index': jax.random.randint(ks[1], (2, E), 0, N), 'edge_type': jax.random.randint(ks[2], (E,), 0, R), 'rel1': w(ks[3], (R, D)), 'W_in1': w(ks[4], (D, D)), 'W_out1': w(ks[5], (D, D)), 'W_loop1': w(ks[6], (D, D)), 'b1': jnp.zeros((D,), jnp.float32), 'rel2': w(ks[7], (R, D)), 'W_in2': w(ks[8], (D, D)), 'W_out2': w(ks[9], (D, D)), 'W_loop2': w(ks[10], (D, D)), 'b2': jnp.zeros((D,), jnp.float32), 'res': jnp.array([0.1], jnp.float32), 'mu_w': w(ks[11], (D, D)), 'mu_b': jnp.zeros((D,), jnp.float32), 'num_nodes': N}
    _L0_gnn_all = _L0_gnn_setup()
    _L0_gnn_in = {k: v for k, v in _L0_gnn_all.items() if k in ('rel1', 'W_in1', 'W_out1', 'W_loop1', 'b1', 'rel2', 'W_in2', 'W_out2', 'W_loop2', 'b2', 'res', 'mu_w', 'mu_b')}
    del _L0_gnn_all

    def _L0_ffn_setup():
        import math
        import jax, jax.numpy as jnp
        import numpy as np
        CAPACITY_FACTOR = 1.25
        TOP_K = 2
        LN_EPS = 1e-05

        def _layer_norm(x, gamma, beta):
            mu = jnp.mean(x, axis=-1, keepdims=True)
            var = jnp.var(x, axis=-1, keepdims=True)
            return (x - mu) * jax.lax.rsqrt(var + LN_EPS) * gamma + beta
        key = jax.random.key(seed)
        ks = jax.random.split(key, 4)
        B, S, D, F, E = (8, 512, 256, 512, 8)
        x = jax.random.normal(ks[0], (B, S, D), dtype=jnp.float32)
        Wr = jax.random.normal(ks[1], (D, E), dtype=jnp.float32) / np.sqrt(D)
        br = jnp.zeros((E,), jnp.float32)
        W1 = jax.random.normal(ks[2], (E, D, F), dtype=jnp.float32) / np.sqrt(D)
        b1 = jnp.zeros((E, F), jnp.float32)
        W2 = jax.random.normal(ks[3], (E, F, D), dtype=jnp.float32) / np.sqrt(F)
        b2 = jnp.zeros((E, D), jnp.float32)
        gamma = jnp.ones((D,), jnp.float32)
        beta = jnp.zeros((D,), jnp.float32)
        return {'x': x, 'Wr': Wr, 'br': br, 'W1': W1, 'b1': b1, 'W2': W2, 'b2': b2, 'gamma': gamma, 'beta': beta}
    _L0_ffn_all = _L0_ffn_setup()
    _L0_ffn_in = {k: v for k, v in _L0_ffn_all.items() if k in ('Wr', 'br', 'W1', 'b1', 'W2', 'b2', 'gamma', 'beta')}
    del _L0_ffn_all
    return {'x': x, 'src': src, 'dst': dst, 'edge_type_400': edge_type_400, 'L0_gnn_rel1': _L0_gnn_in['rel1'], 'L0_gnn_W_in1': _L0_gnn_in['W_in1'], 'L0_gnn_W_out1': _L0_gnn_in['W_out1'], 'L0_gnn_W_loop1': _L0_gnn_in['W_loop1'], 'L0_gnn_b1': _L0_gnn_in['b1'], 'L0_gnn_rel2': _L0_gnn_in['rel2'], 'L0_gnn_W_in2': _L0_gnn_in['W_in2'], 'L0_gnn_W_out2': _L0_gnn_in['W_out2'], 'L0_gnn_W_loop2': _L0_gnn_in['W_loop2'], 'L0_gnn_b2': _L0_gnn_in['b2'], 'L0_gnn_res': _L0_gnn_in['res'], 'L0_gnn_mu_w': _L0_gnn_in['mu_w'], 'L0_gnn_mu_b': _L0_gnn_in['mu_b'], 'L0_ffn_Wr': _L0_ffn_in['Wr'], 'L0_ffn_br': _L0_ffn_in['br'], 'L0_ffn_W1': _L0_ffn_in['W1'], 'L0_ffn_b1': _L0_ffn_in['b1'], 'L0_ffn_W2': _L0_ffn_in['W2'], 'L0_ffn_b2': _L0_ffn_in['b2'], 'L0_ffn_gamma': _L0_ffn_in['gamma'], 'L0_ffn_beta': _L0_ffn_in['beta']}

def reference(x, src, dst, edge_type_400, L0_gnn_rel1, L0_gnn_W_in1, L0_gnn_W_out1, L0_gnn_W_loop1, L0_gnn_b1, L0_gnn_rel2, L0_gnn_W_in2, L0_gnn_W_out2, L0_gnn_W_loop2, L0_gnn_b2, L0_gnn_res, L0_gnn_mu_w, L0_gnn_mu_b, L0_ffn_Wr, L0_ffn_br, L0_ffn_W1, L0_ffn_b1, L0_ffn_W2, L0_ffn_b2, L0_ffn_gamma, L0_ffn_beta):
    import jax
    import jax.numpy as jnp

    def _L0_gnn_ref(emb, edge_index, edge_type, rel1, W_in1, W_out1, W_loop1, b1, rel2, W_in2, W_out2, W_loop2, b2, res, mu_w, mu_b, num_nodes):
        import jax, jax.numpy as jnp
        import numpy as np
        N = 6250
        D = 256
        E = 40000
        R = 400

        def _mgcn_conv(x, edge_index, edge_type, rel, W_in, W_out, W_loop, b, n):
            src, dst = (edge_index[0], edge_index[1])
            e = edge_index.shape[1]
            half = e // 2
            m = x[src] * rel[edge_type]
            m = jnp.concatenate([m[:half] @ W_in, m[half:] @ W_out], 0)
            deg = jax.ops.segment_sum(jnp.ones((e,), x.dtype), dst, num_segments=n)
            norm = 1.0 / jnp.maximum(deg, 1.0)
            agg = jax.ops.segment_sum(m * norm[dst][:, None], dst, num_segments=n)
            return jnp.tanh(agg + x @ W_loop + b)
        h = emb + res * _mgcn_conv(emb, edge_index, edge_type, rel1, W_in1, W_out1, W_loop1, b1, num_nodes)
        h = h + res * _mgcn_conv(h, edge_index, edge_type, rel2, W_in2, W_out2, W_loop2, b2, num_nodes)
        return h @ mu_w + mu_b

    def _L0_ffn_ref(x, Wr, br, W1, b1, W2, b2, gamma, beta):
        import math
        import jax, jax.numpy as jnp
        import numpy as np
        CAPACITY_FACTOR = 1.25
        TOP_K = 2
        LN_EPS = 1e-05

        def _layer_norm(x, gamma, beta):
            mu = jnp.mean(x, axis=-1, keepdims=True)
            var = jnp.var(x, axis=-1, keepdims=True)
            return (x - mu) * jax.lax.rsqrt(var + LN_EPS) * gamma + beta
        B, S, D = x.shape
        E = Wr.shape[1]
        N = B * S
        K = TOP_K
        logits = jnp.mean(x, axis=1) @ Wr + br
        routing_weights = jax.nn.softmax(logits, axis=-1)
        capacity = float(math.ceil(N * CAPACITY_FACTOR / E))
        expected_loads = routing_weights.sum(axis=0) * (N / B)
        scale = jnp.where(expected_loads > capacity, capacity / expected_loads, 1.0)
        routing_weights = jax.nn.softmax(routing_weights * scale, axis=-1)
        rw_tok = jnp.broadcast_to(routing_weights[:, None, :], (B, S, E)).reshape(N, E)
        top_w, top_i = jax.lax.top_k(rw_tok, K)
        top_w = jax.nn.softmax(top_w, axis=-1)
        xf = x.reshape(N, D)
        h = jax.nn.gelu(jnp.einsum('nd,edf->enf', xf, W1) + b1[:, None, :], approximate=False)
        y = jnp.einsum('enf,efd->end', h, W2) + b2[:, None, :]
        w_dense = jnp.zeros((N, E), x.dtype).at[jnp.arange(N)[:, None], top_i].add(top_w)
        out = jnp.einsum('ne,end->nd', w_dense, y).reshape(B, S, D)
        out = _layer_norm(out + x, gamma, beta)
        return out
    edge_index = jnp.stack([src, dst])
    x = x + _L0_gnn_ref(_layernorm(x, axis=-1), edge_index, edge_type_400, L0_gnn_rel1, L0_gnn_W_in1, L0_gnn_W_out1, L0_gnn_W_loop1, L0_gnn_b1, L0_gnn_rel2, L0_gnn_W_in2, L0_gnn_W_out2, L0_gnn_W_loop2, L0_gnn_b2, L0_gnn_res, L0_gnn_mu_w, L0_gnn_mu_b, 6250)
    x = x + _L0_ffn_ref(_layernorm(x, axis=-1)[None], L0_ffn_Wr, L0_ffn_br, L0_ffn_W1, L0_ffn_b1, L0_ffn_W2, L0_ffn_b2, L0_ffn_gamma, L0_ffn_beta)[0]
    return x

_drawn_inputs = setup_inputs


def setup_inputs(seed=0):
    import zlib

    import numpy as np

    out = dict(_drawn_inputs(seed))
    spreads = {'L0_gnn_b1': (0.0, 2.0),
     'L0_gnn_b2': (0.0, 0.8),
     'L0_gnn_mu_b': (0.0, 0.1),
     'L0_ffn_br': (0.0, 0.8),
     'L0_ffn_b1': (0.0, 0.421),
     'L0_ffn_b2': (0.0, 0.284),
     'L0_ffn_gamma': (1.0, 0.2),
     'L0_ffn_beta': (0.0, 0.1)}
    factors = {'L0_gnn_rel1': 8.0,
     'L0_gnn_W_in1': 27.916,
     'L0_gnn_W_out1': 28.222,
     'L0_gnn_rel2': 8.0,
     'L0_gnn_W_in2': 28.376,
     'L0_gnn_W_out2': 28.462,
     'L0_ffn_Wr': 8.0,
     'L0_gnn_W_loop1': 2.714,
     'L0_gnn_W_loop2': 2.748}
    for name, (base, spread) in spreads.items():
        noise = np.random.default_rng([zlib.crc32(name.encode()), seed]).standard_normal(out[name].shape)
        drawn = base * np.exp(spread * noise) if base else spread * noise
        out[name] = jnp.asarray(drawn.astype(out[name].dtype))
    for name, factor in factors.items():
        out[name] = (out[name] * factor).astype(out[name].dtype)
    return out
```

```python
from contextlib import ExitStack

import concourse.bass as bass
from concourse import mybir

ALU = mybir.AluOpType
ACT = mybir.ActivationFunctionType
F32 = mybir.dt.float32
I32 = mybir.dt.int32
U32 = mybir.dt.uint32
AX_X = mybir.AxisListType.X
ds = bass.ds

P = 128
NODES, DIM = 6250, 256
DC = DIM // P
CHUNK = 2 * P
CHUNKS = -(-NODES // CHUNK)
NODES_PAD = CHUNKS * CHUNK
EDGES = 106250
HALF = EDGES // 2
GROUP = 4
RING = 16
GROUPS_IN_RING = RING // GROUP
TILES_HALF = -(-HALF // (P * RING)) * RING
TILES = 2 * TILES_HALF
GROUPS = TILES // GROUP
STEPS = TILES // RING
WIN = 64
WINDOWS = -(-NODES // WIN)
ACC_W = NODES_PAD
assert NODES - 1 + WIN <= ACC_W
FAR = 16384
RELS = 400
HID = 512
HC = HID // P
EXPERTS = 8
TOP = 2
EPS = 1e-5
CAPACITY = float(-(-NODES * 5 // (4 * EXPERTS)))


def wait_past(eng, sem, value):
    if not isinstance(value, int) or value > 0:
        eng.wait_ge(sem, value)


def wait_apart(eng, sem, value, passed):
    if not isinstance(value, int) or value > 0:
        eng.wait_ge(sem, value)
        eng.sem_inc(passed, 1)


def over_chunks(eng, *stages):
    def turn(c, half, par):
        for lag, stage in stages:
            if isinstance(c, int):
                if 0 <= c - lag < CHUNKS:
                    stage(c - lag, (c - lag) % 2, (c - lag) // 2)
            else:
                stage(c - lag, (par - lag) % 2, half - (1 if par < lag else 0) if lag < 2 else half - 1)

    last = max(lag for lag, _ in stages)
    apart = 4 if last else 2
    for c in range(apart):
        turn(c, c // 2, c % 2)
    with eng.Fori(apart // 2, CHUNKS // 2) as i:
        turn(2 * i, i, 0)
        turn(2 * i + 1, i, 1)
    for c in range(CHUNKS // 2 * 2, CHUNKS + last):
        turn(c, c // 2, c % 2)


class Scope:

    def __init__(self, nc, ctx, name):
        self.nc, self.ctx, self.name = nc, ctx, name

    def sb(self, name, shape, dt=F32):
        return self.ctx.enter_context(self.nc.sbuf_tensor(f"{self.name}_{name}", shape, dt))

    def ps(self, name, shape, dt=F32):
        return self.ctx.enter_context(self.nc.psum_tensor(f"{self.name}_{name}", shape, dt))

    def sem(self, name):
        return self.ctx.enter_context(self.nc.semaphore(f"{self.name}_{name}"))


def rows_of(dram, c):
    return dram[ds(c * CHUNK, CHUNK), :].rearrange("(j p) d -> p j d", p=P)


def transposed(K, c, k):
    return K["acc"][:].rearrange("p n k -> p (n k)")[:, ds((c * DC + k) * CHUNK, CHUNK)]


def phase_setup(nc, K, x, dst_tiles, res, emb, emb_t):
    with ExitStack() as ctx:
        s = Scope(nc, ctx, "set")
        dst_i = s.sb("dst_i", [P, TILES], I32)
        neg = s.sb("neg", [P, TILES])
        real = s.sb("real", [P, TILES])
        neg_max = s.sb("neg_max", [P, TILES])
        real_max = s.sb("real_max", [P, TILES])
        gmin = s.sb("gmin", [P, GROUPS])
        gmax = s.sb("gmax", [P, GROUPS])
        half_at = s.sb("half_at", [P, GROUPS])
        acc_at = s.sb("acc_at", [P, GROUPS])
        span = s.sb("span", [P, GROUPS])
        span_max = s.sb("span_max", [P, 1])
        x_rows = s.sb("x_rows", [P, 2, 2, DIM])
        e_rows = s.sb("e_rows", [P, 2, 2, DIM])
        e_t = s.sb("e_t", [P, 2, DC, CHUNK])
        stats = s.sb("stats", [P, 2, 2, 6])
        mv = s.sb("mv", [P, 2, 2, 2])
        rstd = s.sb("rstd", [P, 2, 2])
        tr = [s.ps(f"tr{b}", [P, DC, CHUNK]) for b in range(2)]

        dst_in = s.sem("dst_in")
        res_in = s.sem("res_in")
        consts = s.sem("consts")
        zeroed = s.sem("zeroed")
        chain = s.sem("chain")
        reduced = s.sem("reduced")
        x_in = [s.sem(f"x_in{b}") for b in range(2)]
        stats_done = s.sem("stats_done")
        mv_done = s.sem("mv_done")
        rstd_half = s.sem("rstd_half")
        rstd_done = s.sem("rstd_done")
        emb_done = s.sem("emb_done")
        tr_done = s.sem("tr_done")
        copied = s.sem("copied")
        rows_out = [s.sem(f"rows_out{b}") for b in range(2)]
        t_out = [s.sem(f"t_out{b}") for b in range(2)]
        passed = s.sem("passed")
        block = ctx.enter_context(nc.Block())

        @block.sync
        def _(sp):
            sp.dma_start(dst_i[:], dst_tiles).then_inc(dst_in, 16)
            sp.dma_start(K["res"][:], res.partition_broadcast(P)).then_inc(res_in, 16)

            def load(c, b, n):
                wait_past(sp, emb_done, c - 1)
                sp.dma_start(x_rows[:, b], rows_of(x, c)).then_inc(x_in[b], 16)

            def store(c, b, n):
                sp.wait_ge(emb_done, c + 1)
                sp.dma_start(rows_of(emb, c), e_rows[:, b]).then_inc(rows_out[b], 16)
                sp.wait_ge(copied, c + 1)
                sp.dma_start(emb_t[ds(c, 1)].rearrange("o p f -> p (o f)"),
                             e_t[:, b].rearrange("p k n -> p (k n)")).then_inc(t_out[b], 16)

            over_chunks(sp, (0, load), (1, store))
            sp.wait_ge(res_in, 16)
            for b in range(2):
                sp.wait_ge(rows_out[b], 16 * ((CHUNKS + 1 - b) // 2))
                sp.wait_ge(t_out[b], 16 * ((CHUNKS + 1 - b) // 2))

        @block.gpsimd
        def _(pool):
            pool.memset(K["ident"][:], 0.0).then_inc(consts, 1)
            pool.memset(K["ones"][:], 1.0).then_inc(consts, 1)
            pool.memset(K["minus_half"][:], -0.5).then_inc(consts, 1)
            pool.memset(K["eps"][:], EPS).then_inc(consts, 1)
            pool.memset(K["zeros"][:], 0.0).then_inc(consts, 1)
            pool.iota(K["node_iota"][:], [[1, WIN]], base=0, channel_multiplier=0,
                      allow_small_or_imprecise_dtypes=True).then_inc(consts, 1)
            pool.iota(half_at[:], [[ACC_W, 2], [0, GROUPS // 2]], base=0, channel_multiplier=0,
                      allow_small_or_imprecise_dtypes=True).then_inc(consts, 1)
            pool.wait_ge(consts, 7)
            pool.affine_select(out=K["ident"][:], in_=K["ident"][:], compare_op=ALU.not_equal, fill=1.0,
                               base=0, pattern=[[-1, P]], channel_multiplier=1).then_inc(consts, 1)

            def inverse_deviation(c, b, n):
                pool.wait_ge(mv_done, 2 * c + 2)
                wait_past(pool, emb_done, c - 1)
                pool.tensor_tensor(rstd[:, b], mv[:, b, :, 1], K["eps"][:], ALU.add).then_inc(rstd_half, 1)
                pool.wait_ge(rstd_half, c + 1)
                pool.tensor_tensor(rstd[:, b], rstd[:, b], K["minus_half"][:, 0:2], ALU.pow).then_inc(rstd_done, 1)

            over_chunks(pool, (0, inverse_deviation))
            pool.wait_ge(chain, 3)
            pool.partition_all_reduce(neg_max[:], neg[:], P, bass.bass_isa.ReduceOp.max).then_inc(reduced, 1)
            pool.partition_all_reduce(real_max[:], real[:], P, bass.bass_isa.ReduceOp.max).then_inc(reduced, 1)

        @block.vector
        def _(dve):
            dve.wait_ge(dst_in, 16)
            dve.tensor_copy(K["dst"][:], dst_i[:]).then_inc(chain, 1)
            dve.wait_ge(chain, 1)
            dve.tensor_scalar(neg[:], K["dst"][:], -1.0, None, ALU.mult).then_inc(chain, 1)
            dve.scalar_tensor_tensor(real[:], K["dst"][:], float(FAR), K["dst"][:],
                                     ALU.is_lt, ALU.mult).then_inc(chain, 1)

            def moments(c, b, n):
                dve.wait_ge(x_in[b], 16 * (n + 1))
                for j in range(2):
                    dve.bn_stats(stats[:, b, j], x_rows[:, b, j]).then_inc(stats_done, 1)
                wait_past(dve, emb_done, c - 1)
                for j in range(2):
                    wait_apart(dve, stats_done, 2 * c + 1 + j, passed)
                    dve.bn_aggr(mv[:, b, j], stats[:, b, j]).then_inc(mv_done, 1)

            def normalize(c, b, n):
                dve.wait_ge(rstd_done, c + 1)
                wait_past(dve, rows_out[b], 16 * n)
                wait_past(dve, tr_done, c - 1)
                for j in range(2):
                    ins = dve.tensor_scalar(e_rows[:, b, j], x_rows[:, b, j], mv[:, b, j, 0:1],
                                            rstd[:, b, j:j + 1], ALU.subtract, ALU.mult)
                ins.then_inc(emb_done, 1)

            over_chunks(dve, (0, moments), (1, normalize))

            dve.wait_ge(reduced, 2)
            dve.wait_ge(consts, 8)
            dve.tensor_reduce(gmin[:], neg_max[:].rearrange("p (g t) -> p g t", t=GROUP), AX_X,
                              ALU.max).then_inc(chain, 1)
            dve.tensor_reduce(gmax[:], real_max[:].rearrange("p (g t) -> p g t", t=GROUP), AX_X,
                              ALU.max).then_inc(chain, 1)
            dve.wait_ge(chain, 5)
            dve.tensor_tensor(span[:], gmax[:], gmin[:], ALU.add).then_inc(chain, 1)
            dve.tensor_tensor(K["dst_rel"][:].rearrange("p (g t) -> p g t", t=GROUP),
                              K["dst"][:].rearrange("p (g t) -> p g t", t=GROUP),
                              gmin[:].unsqueeze(2).to_broadcast([P, GROUPS, GROUP]), ALU.add).then_inc(chain, 1)
            dve.tensor_scalar(K["base"][:], gmin[:], -1.0, None, ALU.mult).then_inc(chain, 1)
            dve.tensor_tensor(acc_at[:], half_at[:], gmin[:], ALU.subtract).then_inc(chain, 1)
            dve.tensor_copy(K["half_at"][:], half_at[:]).then_inc(chain, 1)
            dve.wait_ge(chain, 10)
            dve.tensor_copy(K["acc_at"][:], acc_at[:]).then_inc(chain, 1)
            dve.tensor_reduce(span_max[:], span[:], AX_X, ALU.max).then_inc(chain, 1)
            dve.wait_ge(chain, 12)
            dve.tensor_copy(K["span"][:], span_max[:]).then_inc(chain, 1)
            dve.memset(K["deg"][:], 0.0).then_inc(zeroed, 1)
            dve.memset(K["acc"][:], 0.0).then_inc(zeroed, 1)

        @block.tensor
        def _(pe):
            pe.wait_ge(consts, 8)

            def transpose(c, b, n):
                pe.wait_ge(emb_done, c + 1)
                wait_past(pe, copied, c - 1)
                for k in range(DC):
                    for j in range(2):
                        ins = pe.transpose(tr[b][:, k, j * P:(j + 1) * P],
                                           e_rows[:, b, j, k * P:(k + 1) * P], K["ident"][:])
                ins.then_inc(tr_done, 1)

            over_chunks(pe, (0, transpose))

        @block.scalar
        def _(act):
            def copy(c, b, n):
                act.wait_ge(tr_done, c + 1)
                wait_past(act, t_out[b], 16 * n)
                act.copy(e_t[:, b], tr[b][:]).then_inc(copied, 1)

            over_chunks(act, (0, copy))


def phase_edges(nc, K, layer, nodes, rel, src_idx, type_idx, rel_kept):
    first = layer == 0
    with ExitStack() as ctx:
        s = Scope(nc, ctx, f"edge{layer}")
        xg = s.sb("xg", [P, RING, DIM])
        rg = s.sb("rg", [P, RING, 2 * DIM if first else DIM])
        sel = s.sb("sel", [P, RING, WIN])
        src_i = s.sb("src_i", [P, 2, RING // 2], I32)
        typ_i = s.sb("typ_i", [P, 2, RING // 2], I32)
        shifted = s.sb("shifted", [P, GROUP])
        win_base = s.sb("win_base", [P, 1])
        sums = [s.ps(f"sums{b}", [P, DC + 1, WIN]) for b in range(2)]

        idx_in = [s.sem(f"idx_in{b}") for b in range(2)]
        gathered = [s.sem(f"gathered{q}") for q in range(GROUPS_IN_RING)]
        rel_moved = [s.sem(f"rel_moved{q}") for q in range(GROUPS_IN_RING)]
        selected = s.sem("selected")
        messages = s.sem("messages")
        group_summed = s.sem("group_summed")
        acc_added = s.sem("acc_added")
        deg_added = s.sem("deg_added")
        win_step = s.sem("win_step")
        win_selected = s.sem("win_selected")
        win_summed = s.sem("win_summed")
        win_added = s.sem("win_added")
        win_deg = s.sem("win_deg")
        passed = s.sem("passed")
        block = ctx.enter_context(nc.Block())
        gathers = 2 * GROUP if first else GROUP

        def steps(eng, body):
            body(0)
            with eng.Fori(1, STEPS) as i:
                body(i)

        def block_idx(dram, i, h):
            return dram[ds(2 * i + h, 1)].rearrange("o p k -> p (o k)")

        @block.sync
        def _(sp):
            def load(i):
                for h in range(2):
                    for q in range(h * GROUPS_IN_RING // 2, (h + 1) * GROUPS_IN_RING // 2):
                        wait_past(sp, gathered[q], 16 * gathers * i)
                    sp.dma_start(src_i[:, h], block_idx(src_idx, i, h)).then_inc(idx_in[h], 16)
                    sp.dma_start(typ_i[:, h], block_idx(type_idx, i, h)).then_inc(idx_in[h], 16)

            steps(sp, load)

        @block.gpsimd
        def _(pool):
            def gather(i):
                for q in range(GROUPS_IN_RING):
                    g = GROUPS_IN_RING * i + q
                    if q % 2 == 0:
                        wait_apart(pool, idx_in[q // 2], 32 * (i + 1), passed)
                    if first:
                        wait_past(pool, rel_moved[q], 16 * i)
                    wait_apart(pool, group_summed, g + 1 - GROUPS_IN_RING, passed)
                    for t in range(GROUP * q, GROUP * q + GROUP):
                        h, k = t // (RING // 2), t % (RING // 2)
                        pool.indirect_dma_start(
                            xg[:, t, :], None, nodes,
                            bass.IndirectOffsetOnAxis(ap=src_i[:, h, k:k + 1], axis=0)).then_inc(gathered[q], 16)
                        if first:
                            pool.indirect_dma_start(
                                rg[:, t, :], None, rel,
                                bass.IndirectOffsetOnAxis(ap=typ_i[:, h, k:k + 1], axis=0)).then_inc(gathered[q], 16)

            steps(pool, gather)

        @block.scalar
        def _(act):
            def move(i):
                for q in range(GROUPS_IN_RING):
                    g = GROUPS_IN_RING * i + q
                    kept = rel_kept[ds(g, 1)].rearrange("o p t d -> p (o t) d")
                    part = rg[:, GROUP * q:GROUP * (q + 1), :]
                    if first:
                        act.wait_ge(gathered[q], 16 * gathers * (i + 1))
                        act.dma_start(kept, part[:, :, DIM:]).then_inc(rel_moved[q], 16)
                    else:
                        wait_past(act, messages, g + 1 - GROUPS_IN_RING)
                        act.dma_start(part, kept).then_inc(rel_moved[q], 16)

            steps(act, move)
            for q in range(GROUPS_IN_RING):
                act.wait_ge(rel_moved[q], 16 * STEPS)

        @block.vector
        def _(dve):
            def message(i, q):
                g = GROUPS_IN_RING * i + q
                at = slice(GROUP * q, GROUP * (q + 1))
                dve.wait_ge(gathered[q], 16 * gathers * (i + 1))
                if not first:
                    dve.wait_ge(rel_moved[q], 16 * (i + 1))
                dve.tensor_tensor(xg[:, at, :], xg[:, at, :], rg[:, at, 0:DIM], ALU.mult).then_inc(messages, 1)

            def select(out, dst):
                return dve.tensor_tensor(out, K["node_iota"][:].unsqueeze(1).to_broadcast([P, GROUP, WIN]),
                                         dst.unsqueeze(2).to_broadcast([P, GROUP, WIN]), ALU.is_equal)

            def add(g, b, base, acc_at, added, counted):
                part = K["acc"][:, ds(acc_at, WIN), :]
                dve.tensor_tensor(part, part, sums[b][:, 0:DC, :].rearrange("p k n -> p n k"),
                                  ALU.add).then_inc(added, 1)
                if first:
                    part = K["deg"][:, ds(base, WIN)]
                    dve.tensor_tensor(part, part, sums[b][:, DC, :], ALU.add).then_inc(counted, 1)

            def short(_=None):
                def added(g, b):
                    base = dve.value_load(K["base"][0:1, ds(g, 1)], min_val=0, max_val=ACC_W - WIN) if first else None
                    acc_at = dve.value_load(K["acc_at"][0:1, ds(g, 1)], min_val=0, max_val=2 * ACC_W - WIN)
                    dve.wait_ge(group_summed, g + 1)
                    wait_past(dve, acc_added, g)
                    if first:
                        wait_past(dve, deg_added, g)
                    add(g, b, base, acc_at, acc_added, deg_added)

                def step(i):
                    for q in range(GROUPS_IN_RING):
                        g = GROUPS_IN_RING * i + q
                        wait_past(dve, group_summed, g + 1 - GROUPS_IN_RING)
                        select(sel[:, GROUP * q:GROUP * (q + 1), :],
                               K["dst_rel"][:, ds(GROUP * g, GROUP)]).then_inc(selected, 1)
                        message(i, q)
                        if not isinstance(g, int) or g > 0:
                            added(g - 1, (q - 1) % 2)

                steps(dve, step)
                added(GROUPS - 1, 1)

            def long():
                dve.sem_inc(win_added, 1)
                if first:
                    dve.sem_inc(win_deg, 1)

                def step(i):
                    for q in range(GROUPS_IN_RING):
                        g = GROUPS_IN_RING * i + q
                        message(i, q)
                        half_at = dve.value_load(K["half_at"][0:1, ds(g, 1)], min_val=0, max_val=ACC_W)
                        dve.memset(win_base[:], -float(WIN)).then_inc(win_step, 1)
                        with dve.Fori(0, WINDOWS) as w:
                            n = g * WINDOWS + w
                            dve.wait_ge(win_step, g * (2 * WINDOWS + 1) + 2 * w + 1)
                            dve.tensor_scalar(win_base[:], win_base[:], float(WIN), None, ALU.add).then_inc(win_step, 1)
                            dve.wait_ge(win_step, g * (2 * WINDOWS + 1) + 2 * w + 2)
                            dve.tensor_scalar(shifted[:], K["dst"][:, ds(GROUP * g, GROUP)], win_base[:, 0:1], None,
                                              ALU.subtract).then_inc(win_step, 1)
                            dve.wait_ge(win_step, g * (2 * WINDOWS + 1) + 2 * w + 3)
                            select(sel[:, GROUP * q:GROUP * (q + 1), :], shifted[:]).then_inc(win_selected, 1)
                            dve.wait_ge(win_summed, n + 1)
                            add(g, 0, w * WIN, half_at + w * WIN, win_added, win_deg)

                steps(dve, step)
                dve.wait_ge(win_added, GROUPS * WINDOWS + 1)

            wide = dve.value_load(K["span"][0:1, 0:1], min_val=0, max_val=2 * FAR)
            with dve.If(wide < WIN):
                short()
            with dve.Else():
                long()

        @block.tensor
        def _(pe):
            def sum_window(q, b):
                for k in range(DC + 1 if first else DC):
                    for t in range(GROUP):
                        at = GROUP * q + t
                        lhs = xg[:, at, k * P:(k + 1) * P] if k < DC else K["ones"][:]
                        ins = pe.matmul(sums[b][:, k, :], lhs, sel[:, at, :], start=(t == 0), stop=(t == GROUP - 1))
                return ins

            def short():
                def step(i):
                    for q in range(GROUPS_IN_RING):
                        g = GROUPS_IN_RING * i + q
                        pe.wait_ge(selected, g + 1)
                        pe.wait_ge(messages, g + 1)
                        wait_past(pe, acc_added, g - 1)
                        if first:
                            wait_past(pe, deg_added, g - 1)
                        sum_window(q, q % 2).then_inc(group_summed, 1)

                steps(pe, step)

            def long():
                def step(i):
                    for q in range(GROUPS_IN_RING):
                        g = GROUPS_IN_RING * i + q
                        wait_apart(pe, messages, g + 1, passed)
                        with pe.Fori(0, WINDOWS) as w:
                            n = g * WINDOWS + w
                            pe.wait_ge(win_selected, n + 1)
                            pe.wait_ge(win_added, n + 1)
                            if first:
                                pe.wait_ge(win_deg, n + 1)
                            sum_window(q, 0).then_inc(win_summed, 1)
                        pe.wait_ge(win_added, (g + 1) * WINDOWS + 1)
                        pe.sem_inc(group_summed, 1)

                steps(pe, step)

            wide = pe.value_load(K["span"][0:1, 0:1], min_val=0, max_val=2 * FAR)
            with pe.If(wide < WIN):
                short()
            with pe.Else():
                long()


def phase_dense(nc, K, layer, prev_t, next_t, next_rows, W_in, W_out, W_loop, b, tail=None):
    first = layer == 0
    with ExitStack() as ctx:
        s = Scope(nc, ctx, f"dense{layer}")
        w_sb = s.sb("w", [P, 3, DC, DIM])
        b_sb = s.sb("b", [P, DC])
        prev = s.sb("prev", [P, 2, DC, CHUNK])
        scaled = s.sb("scaled", [P, 2, 2, DC, CHUNK])
        th = s.sb("th", [P, 2, DC, CHUNK])
        h_t = s.sb("h_t", [P, 2, DC, CHUNK])
        lin = [s.ps(f"lin{k}", [P, DC, CHUNK]) for k in range(2)]
        tr = [s.ps(f"tr{k}", [P, 2, DIM]) for k in range(2)]
        rows = s.sb("rows", [P, 2, 2, DIM])

        w_in = s.sem("w_in")
        prev_in = [s.sem(f"prev_in{k}") for k in range(2)]
        clamped = s.sem("clamped")
        normed = s.sem("normed")
        scaled_done = s.sem("scaled_done")
        cleared = s.sem("cleared")
        lin_done = s.sem("lin_done")
        tanh_done = s.sem("tanh_done")
        h_done = s.sem("h_done")
        tr_done = s.sem("tr_done")
        rows_done = s.sem("rows_done")
        rows_out = [s.sem(f"rows_out{k}") for k in range(2)]
        t_out = [s.sem(f"t_out{k}") for k in range(2)]
        if not first:
            x, mu_w, mu_b, x2_dram, xl_dram = tail
            mu_sb = s.sb("mu_w", [P, DC, DIM])
            mub_sb = s.sb("mu_b", [P, DIM])
            xb = s.sb("xb", [P, 2, 2, DIM])
            x2 = s.sb("x2", [P, 2, 2, DIM])
            stats = s.sb("stats", [P, 2, 2, 6])
            mv = s.sb("mv", [P, 2, 2, 2])
            rstd = s.sb("rstd", [P, 2, 2])
            mu = [s.ps(f"mu{k}", [P, 2, DIM]) for k in range(2)]
            x_in = [s.sem(f"x_in{k}") for k in range(2)]
            xb_done = s.sem("xb_done")
            mu_done = s.sem("mu_done")
            x2_done = s.sem("x2_done")
            stats_done = s.sem("stats_done")
            mv_done = s.sem("mv_done")
            rstd_half = s.sem("rstd_half")
            rstd_done = s.sem("rstd_done")
            cols_done = s.sem("cols_done")
            x2_out = [s.sem(f"x2_out{k}") for k in range(2)]
        n_w = 3 + 1 + (0 if first else 2)
        passed = s.sem("passed")
        block = ctx.enter_context(nc.Block())

        @block.sync
        def _(sp):
            for k, w in enumerate((W_in, W_out, W_loop)):
                sp.dma_start(w_sb[:, k], w.rearrange("(c p) m -> p c m", p=P)).then_inc(w_in, 16)
            sp.dma_start(b_sb[:], b.rearrange("(c p) -> p c", p=P),
                         allow_slow_non_contiguous=True).then_inc(w_in, 16)
            if not first:
                sp.dma_start(mu_sb[:], mu_w.rearrange("(c p) m -> p c m", p=P)).then_inc(w_in, 16)
                sp.dma_start(mub_sb[:], mu_b.partition_broadcast(P)).then_inc(w_in, 16)

            def load(c, b, n):
                wait_past(sp, h_done, c - 1)
                sp.dma_start(prev[:, b].rearrange("p k n -> p (k n)"),
                             prev_t[ds(c, 1)].rearrange("o p f -> p (o f)")).then_inc(prev_in[b], 16)
                if not first:
                    wait_past(sp, x2_done, c - 1)
                    sp.dma_start(xb[:, b], rows_of(x, c)).then_inc(x_in[b], 16)

            def store_t(c, b, n):
                sp.wait_ge(h_done, c + 1)
                sp.dma_start(next_t[ds(c, 1)].rearrange("o p f -> p (o f)"),
                             h_t[:, b].rearrange("p k n -> p (k n)")).then_inc(t_out[b], 16)

            def store_rows(c, b, n):
                sp.wait_ge(rows_done, c + 1)
                sp.dma_start(rows_of(next_rows, c), rows[:, b]).then_inc(rows_out[b], 16)

            def store_x2(c, b, n):
                sp.wait_ge(x2_done, c + 1)
                sp.dma_start(rows_of(x2_dram, c), x2[:, b]).then_inc(x2_out[b], 16)
                sp.wait_ge(rows_done, c + 1)
                sp.dma_start(rows_of(xl_dram, c), rows[:, b]).then_inc(rows_out[b], 16)

            if first:
                over_chunks(sp, (0, load), (1, store_t), (2, store_rows))
            else:
                over_chunks(sp, (0, load), (2, store_x2))
            for k in range(2):
                times = (CHUNKS + 1 - k) // 2
                sp.wait_ge(rows_out[k], 16 * times)
                sp.wait_ge(t_out[k] if first else x2_out[k], 16 * times)

        @block.gpsimd
        def _(pool):
            if first:
                def clear(c, b, n):
                    pool.wait_ge(scaled_done, 2 * c + 2)
                    for h in range(2):
                        pool.tensor_copy(K["acc"][:, ds(h * ACC_W + c * CHUNK, CHUNK), :], K["zeros"][:]).then_inc(cleared, 1)

                over_chunks(pool, (0, clear))
                return
            pool.wait_ge(w_in, 16 * n_w)

            def add_bias(c, b, n):
                pool.wait_ge(x_in[b], 16 * (n + 1))
                pool.tensor_tensor(xb[:, b], xb[:, b], mub_sb[:].unsqueeze(1).to_broadcast([P, 2, DIM]),
                                   ALU.add).then_inc(xb_done, 1)

            def inverse_deviation(c, b, n):
                pool.wait_ge(mv_done, 2 * c + 2)
                wait_past(pool, rows_done, c - 1)
                pool.tensor_tensor(rstd[:, b], mv[:, b, :, 1], K["eps"][:], ALU.add).then_inc(rstd_half, 1)
                pool.wait_ge(rstd_half, c + 1)
                pool.tensor_tensor(rstd[:, b], rstd[:, b], K["minus_half"][:, 0:2], ALU.pow).then_inc(rstd_done, 1)

            over_chunks(pool, (0, add_bias), (2, inverse_deviation))

        @block.vector
        def _(dve):
            def scale(c, b, n):
                norm = K["deg"][:, ds(c * CHUNK, CHUNK)]
                if first:
                    dve.tensor_scalar(norm, norm, 1.0, None, ALU.max).then_inc(clamped, 1)
                    wait_apart(dve, clamped, c + 1, passed)
                    dve.reciprocal(norm, norm).then_inc(normed, 1)
                    dve.wait_ge(normed, c + 1)
                wait_past(dve, lin_done, c - 1)
                for h in range(2):
                    dve.tensor_tensor(
                        scaled[:, b, h],
                        K["acc"][:, ds(h * ACC_W + c * CHUNK, CHUNK), :].rearrange("p n k -> p k n"),
                        norm.unsqueeze(1).to_broadcast([P, DC, CHUNK]), ALU.mult).then_inc(scaled_done, 1)

            def residual(c, b, n):
                dve.wait_ge(tanh_done, 2 * c + 2)
                if first:
                    wait_past(dve, tr_done, c - 1)
                    wait_past(dve, t_out[b], 16 * n)
                else:
                    wait_past(dve, mu_done, c - 1)
                dve.scalar_tensor_tensor(h_t[:, b], th[:, b], K["res"][:, 0:1], prev[:, b], ALU.mult,
                                         ALU.add).then_inc(h_done, 1)

            def second_norm(c, b, n):
                dve.wait_ge(mu_done, c + 1)
                dve.wait_ge(xb_done, c + 1)
                wait_past(dve, x2_out[b], 16 * n)
                dve.tensor_tensor(x2[:, b], xb[:, b], mu[b][:], ALU.add).then_inc(x2_done, 1)
                dve.wait_ge(x2_done, c + 1)
                for j in range(2):
                    dve.bn_stats(stats[:, b, j], x2[:, b, j]).then_inc(stats_done, 1)
                for j in range(2):
                    wait_apart(dve, stats_done, 2 * c + 1 + j, passed)
                    dve.bn_aggr(mv[:, b, j], stats[:, b, j]).then_inc(mv_done, 1)
                dve.wait_ge(rstd_done, c + 1)
                wait_past(dve, tr_done, c - 1)
                wait_past(dve, rows_out[b], 16 * n)
                for j in range(2):
                    ins = dve.tensor_scalar(rows[:, b, j], x2[:, b, j], mv[:, b, j, 0:1], rstd[:, b, j:j + 1],
                                            ALU.subtract, ALU.mult)
                ins.then_inc(rows_done, 1)

            dve.wait_ge(w_in, 16 * n_w)
            if first:
                over_chunks(dve, (0, scale), (1, residual))
            else:
                over_chunks(dve, (0, scale), (1, residual), (2, second_norm))

        @block.tensor
        def _(pe):
            pe.wait_ge(w_in, 16 * n_w)

            def linear(c, b, n):
                pe.wait_ge(prev_in[b], 16 * (n + 1))
                pe.wait_ge(scaled_done, 2 * c + 2)
                wait_past(pe, tanh_done, 2 * c - 2)
                for m in range(DC):
                    cols = slice(m * P, (m + 1) * P)
                    for k in range(DC):
                        pe.matmul(lin[b][:, m, :], w_sb[:, 2, k, cols], prev[:, b, k], start=(k == 0), stop=False)
                    for h in range(2):
                        for k in range(DC):
                            ins = pe.matmul(lin[b][:, m, :], w_sb[:, h, k, cols], scaled[:, b, h, k],
                                            start=False, stop=(h == 1 and k == DC - 1))
                ins.then_inc(lin_done, 1)

            def to_rows(c, b, n):
                pe.wait_ge(h_done, c + 1)
                wait_past(pe, rows_done, c - 1)
                for j in range(2):
                    for k in range(DC):
                        ins = pe.transpose(tr[b][:, j, k * P:(k + 1) * P], h_t[:, b, k, j * P:(j + 1) * P],
                                           K["ident"][:])
                ins.then_inc(tr_done, 1)

            def project(c, b, n):
                pe.wait_ge(h_done, c + 1)
                wait_past(pe, x2_done, c - 1)
                for j in range(2):
                    for k in range(DC):
                        ins = pe.matmul(mu[b][:, j, :], h_t[:, b, k, j * P:(j + 1) * P], mu_sb[:, k, :],
                                        start=(k == 0), stop=(k == DC - 1))
                ins.then_inc(mu_done, 1)

            def to_columns(c, b, n):
                pe.wait_ge(rows_done, c + 1)
                wait_past(pe, cols_done, 2 * c - 2)
                for k in range(DC):
                    for j in range(2):
                        ins = pe.transpose(tr[b][:, k, j * P:(j + 1) * P], rows[:, b, j, k * P:(k + 1) * P],
                                           K["ident"][:])
                ins.then_inc(tr_done, 1)

            if first:
                over_chunks(pe, (0, linear), (1, to_rows))
            else:
                over_chunks(pe, (0, linear), (1, project), (2, to_columns))

        @block.scalar
        def _(act):
            act.wait_ge(w_in, 16 * n_w)

            def tanh(c, b, n):
                act.wait_ge(lin_done, c + 1)
                wait_past(act, h_done, c - 1)
                for m in range(DC):
                    act.activation(th[:, b, m], lin[b][:, m, :], ACT.Tanh, bias=b_sb[:, m:m + 1]).then_inc(tanh_done, 1)

            def copy_rows(c, b, n):
                act.wait_ge(tr_done, c + 1)
                wait_past(act, rows_out[b], 16 * n)
                act.copy(rows[:, b], tr[b][:]).then_inc(rows_done, 1)

            def copy_columns(c, b, n):
                act.wait_ge(tr_done, c + 1)
                whole = not isinstance(c, int) or (c + 1) * CHUNK <= NODES
                real = CHUNK if whole else NODES - c * CHUNK
                for k in range(DC):
                    act.activation(transposed(K, c, k)[:, 0:real], tr[b][:, k, 0:real], ACT.Copy,
                                   accum_out=K["node_sums"][:, k, ds(c, 1)]).then_inc(cols_done, 1)
                    if not whole:
                        act.copy(transposed(K, c, k)[:, real:], tr[b][:, k, real:]).then_inc(cols_done, 1)

            if first:
                over_chunks(act, (0, tanh), (1, copy_rows))
            else:
                over_chunks(act, (0, tanh), (2, copy_columns))


def phase_ffn(nc, K, x2_dram, xl_dram, Wr, br, W1, b1, W2, b2, gamma, beta, out):
    with ExitStack() as ctx:
        s = Scope(nc, ctx, "ffn")
        area = K["acc"][:].rearrange("p n k -> p (n k)")
        used = NODES_PAD * DC

        def carve(*shape):
            nonlocal used
            size = 1
            for n in shape:
                size *= n
            part = area[:, used:used + size]
            used += size
            if len(shape) == 2:
                return part.rearrange("p (a b) -> p a b", a=shape[0])
            return part.rearrange("p (a b c) -> p a b c", a=shape[0], b=shape[1])

        U = TOP * HC
        w1 = carve(TOP, DC, HID)
        w2 = carve(TOP, HC, DIM)
        hid = carve(2, U, CHUNK)
        b2_sb = carve(TOP, DIM)
        affine = carve(3, DIM)
        xl = s.sb("xl", [P, 2, 2, DIM])
        x2 = s.sb("x2", [P, 2, 2, DIM])
        y = s.sb("y", [P, 2, 2, DIM])
        o = s.sb("o", [P, 2, 2, DIM])
        mean_b = carve(DC, P)
        b1_sb = s.sb("b1", [P, TOP, HC])
        wr_sb = s.sb("wr", [P, DC, EXPERTS])
        br_sb = s.sb("br", [P, EXPERTS])
        mean = s.sb("mean", [P, DC])
        lg = s.sb("lg", [P, EXPERTS])
        ex = s.sb("ex", [P, EXPERTS])
        rw = s.sb("rw", [P, EXPERTS])
        cap = s.sb("cap", [P, EXPERTS])
        one = s.sb("one", [P, 8])
        top = s.sb("top", [P, 8])
        top_i = s.sb("top_i", [P, 8], U32)
        w_top = s.sb("w_top", [P, TOP])
        stats = s.sb("stats", [P, 2, 2, 6])
        mv = s.sb("mv", [P, 2, 2, 2])
        rstd = s.sb("rstd", [P, 2, 2])
        up = [s.ps(f"up{k}", [P, 512]) for k in range(4)]
        down = [s.ps(f"down{k}", [P, 2, DIM]) for k in range(2)]
        route = s.ps("route", [P, 512])

        small_in = s.sem("small_in")
        routed = s.sem("routed")
        mean_ready = s.sem("mean_ready")
        logits_done = s.sem("logits_done")
        shifted = s.sem("shifted")
        exp_done = s.sem("exp_done")
        top_ready = s.sem("top_ready")
        experts_in = s.sem("experts_in")
        weighted = s.sem("weighted")
        rows_in = [s.sem(f"rows_in{k}") for k in range(2)]
        biased = s.sem("biased")
        up_done = s.sem("up_done")
        gelu_done = s.sem("gelu_done")
        down_done = s.sem("down_done")
        y_done = s.sem("y_done")
        stats_done = s.sem("stats_done")
        mv_done = s.sem("mv_done")
        rstd_half = s.sem("rstd_half")
        rstd_done = s.sem("rstd_done")
        z_done = s.sem("z_done")
        g_done = s.sem("g_done")
        o_done = s.sem("o_done")
        stored = [s.sem(f"stored{k}") for k in range(2)]
        passed = s.sem("passed")
        block = ctx.enter_context(nc.Block())

        @block.sync
        def _(sp):
            sp.dma_start(wr_sb[:], Wr.rearrange("(c p) e -> p c e", p=P)).then_inc(small_in, 16)
            sp.dma_start(br_sb[:], br.partition_broadcast(P)).then_inc(small_in, 16)
            sp.dma_start(affine[:, 0], gamma.partition_broadcast(P)).then_inc(small_in, 16)
            sp.dma_start(affine[:, 1], beta.partition_broadcast(P)).then_inc(small_in, 16)
            sp.wait_ge(top_ready, 1)
            for k in range(TOP):
                e = sp.value_load(top_i[0:1, k:k + 1], min_val=0, max_val=EXPERTS - 1)
                sp.dma_start(w1[:, k], W1[ds(e, 1)].rearrange("o (c p) f -> p (o c) f", p=P)).then_inc(experts_in, 16)
                sp.dma_start(w2[:, k], W2[ds(e, 1)].rearrange("o (c p) d -> p (o c) d", p=P)).then_inc(experts_in, 16)
                sp.dma_start(b1_sb[:, k], b1[ds(e, 1)].rearrange("o (c p) -> p (o c)", p=P),
                             allow_slow_non_contiguous=True).then_inc(experts_in, 16)
                sp.dma_start(b2_sb[:, k], b2[ds(e, 1)].rearrange("o d -> (o d)").partition_broadcast(P)).then_inc(experts_in, 16)

            def load(c, b, n):
                wait_past(sp, o_done, c - 1)
                sp.dma_start(xl[:, b], rows_of(xl_dram, c)).then_inc(rows_in[b], 16)
                sp.dma_start(x2[:, b], rows_of(x2_dram, c)).then_inc(rows_in[b], 16)

            def store(c, b, n):
                sp.wait_ge(o_done, c + 1)
                sp.dma_start(rows_of(out, c), o[:, b]).then_inc(stored[b], 16)

            over_chunks(sp, (0, load), (2, store))
            for k in range(2):
                sp.wait_ge(stored[k], 16 * ((CHUNKS + 1 - k) // 2))

        @block.gpsimd
        def _(pool):
            pool.wait_ge(small_in, 64)
            pool.wait_ge(weighted, 4)

            def add_bias(c, b, n):
                pool.wait_ge(rows_in[b], 32 * (n + 1))
                pool.tensor_tensor(xl[:, b], xl[:, b], affine[:, 2].unsqueeze(1).to_broadcast([P, 2, DIM]),
                                   ALU.add).then_inc(biased, 1)
                pool.tensor_tensor(x2[:, b], x2[:, b], affine[:, 1].unsqueeze(1).to_broadcast([P, 2, DIM]),
                                   ALU.add).then_inc(biased, 1)

            def inverse_deviation(c, b, n):
                pool.wait_ge(mv_done, 2 * c + 2)
                wait_past(pool, z_done, 2 * c - 2)
                pool.tensor_tensor(rstd[:, b], mv[:, b, :, 1], K["eps"][:], ALU.add).then_inc(rstd_half, 1)
                pool.wait_ge(rstd_half, c + 1)
                pool.tensor_tensor(rstd[:, b], rstd[:, b], K["minus_half"][:, 0:2], ALU.pow).then_inc(rstd_done, 1)

            over_chunks(pool, (0, add_bias), (0, inverse_deviation))

        @block.vector
        def _(dve):
            links = 0

            def link(ins):
                nonlocal links
                links += 1
                ins.then_inc(routed, 1)
                dve.wait_ge(routed, links)

            link(dve.tensor_reduce(mean[:], K["node_sums"][:], AX_X, ALU.add))
            link(dve.tensor_scalar(mean[:], mean[:], 1.0 / NODES, None, ALU.mult))
            dve.tensor_copy(mean_b, mean[:].unsqueeze(2).to_broadcast([P, DC, P])).then_inc(mean_ready, 1)
            dve.wait_ge(logits_done, 1)
            dve.wait_ge(small_in, 64)
            link(dve.tensor_tensor(lg[:], route[:, 0:EXPERTS], br_sb[:], ALU.add))

            def softmax(turn):
                link(dve.tensor_reduce(one[:, 0:1], lg[:], AX_X, ALU.max))
                dve.tensor_scalar(lg[:], lg[:], one[:, 0:1], None, ALU.subtract).then_inc(shifted, 1)
                dve.wait_ge(exp_done, turn)
                link(dve.tensor_reduce(one[:, 1:2], ex[:], AX_X, ALU.add))
                link(dve.reciprocal(one[:, 2:3], one[:, 1:2]))
                link(dve.tensor_scalar(rw[:], ex[:], one[:, 2:3], None, ALU.mult))

            softmax(1)
            link(dve.tensor_scalar(cap[:], rw[:], float(NODES), CAPACITY, ALU.mult, ALU.max))
            link(dve.reciprocal(cap[:], cap[:]))
            link(dve.tensor_scalar(cap[:], cap[:], CAPACITY, None, ALU.mult))
            link(dve.tensor_tensor(lg[:], rw[:], cap[:], ALU.mult))
            softmax(2)
            link(dve.max(top[:], rw[:]))
            dve.max_index(top_i[:], top[:], rw[:]).then_inc(top_ready, 1)
            dve.tensor_tensor(lg[:, 0:1], top[:, 1:2], top[:, 0:1], ALU.subtract).then_inc(shifted, 1)
            dve.wait_ge(exp_done, 3)
            link(dve.tensor_scalar(one[:, 3:4], ex[:, 0:1], 1.0, None, ALU.add))
            link(dve.reciprocal(w_top[:, 0:1], one[:, 3:4]))
            link(dve.tensor_tensor(w_top[:, 1:2], ex[:, 0:1], w_top[:, 0:1], ALU.mult))
            dve.wait_ge(experts_in, 128)
            for k in range(TOP):
                dve.tensor_scalar(w2[:, k], w2[:, k], w_top[:, k:k + 1], None, ALU.mult).then_inc(weighted, 1)
            dve.tensor_scalar(affine[:, 2], b2_sb[:, 0], w_top[:, 0:1], None, ALU.mult).then_inc(weighted, 1)
            dve.wait_ge(weighted, 3)
            dve.scalar_tensor_tensor(affine[:, 2], b2_sb[:, 1], w_top[:, 1:2], affine[:, 2], ALU.mult,
                                     ALU.add).then_inc(weighted, 1)

            def moments(c, b, n):
                dve.wait_ge(down_done, c + 1)
                dve.wait_ge(biased, 2 * c + 2)
                dve.tensor_tensor(y[:, b], down[b][:], xl[:, b], ALU.add).then_inc(y_done, 1)
                dve.wait_ge(y_done, c + 1)
                for j in range(2):
                    dve.bn_stats(stats[:, b, j], y[:, b, j]).then_inc(stats_done, 1)
                for j in range(2):
                    wait_apart(dve, stats_done, 2 * c + 1 + j, passed)
                    dve.bn_aggr(mv[:, b, j], stats[:, b, j]).then_inc(mv_done, 1)

            def finish(c, b, n):
                dve.wait_ge(rstd_done, c + 1)
                for j in range(2):
                    dve.tensor_scalar(y[:, b, j], y[:, b, j], mv[:, b, j, 0:1], rstd[:, b, j:j + 1],
                                      ALU.subtract, ALU.mult).then_inc(z_done, 1)
                dve.wait_ge(z_done, 2 * c + 2)
                dve.tensor_tensor(y[:, b], y[:, b], affine[:, 0].unsqueeze(1).to_broadcast([P, 2, DIM]),
                                  ALU.mult).then_inc(g_done, 1)
                dve.wait_ge(g_done, c + 1)
                wait_past(dve, stored[b], 16 * n)
                dve.tensor_tensor(o[:, b], y[:, b], x2[:, b], ALU.add).then_inc(o_done, 1)

            over_chunks(dve, (1, finish), (0, moments))

        @block.tensor
        def _(pe):
            pe.wait_ge(mean_ready, 1)
            pe.wait_ge(small_in, 64)
            for k in range(DC):
                ins = pe.matmul(route[:, 0:EXPERTS], mean_b[:, k], wr_sb[:, k], start=(k == 0), stop=(k == DC - 1))
            ins.then_inc(logits_done, 1)
            pe.wait_ge(experts_in, 128)
            pe.wait_ge(weighted, 2)

            def widen(c, b, n):
                for u in range(U):
                    wait_past(pe, gelu_done, U * c + u - 3)
                    for k in range(DC):
                        ins = pe.matmul(up[u % 4][:, 0:CHUNK], w1[:, u // HC, k, (u % HC) * P:(u % HC + 1) * P],
                                        transposed(K, c, k), start=(k == 0), stop=(k == DC - 1))
                    ins.then_inc(up_done, 1)

            def narrow(c, b, n):
                pe.wait_ge(gelu_done, U * (c + 1))
                wait_past(pe, y_done, c - 1)
                for j in range(2):
                    for u in range(U):
                        ins = pe.matmul(down[b][:, j, :], hid[:, b, u, j * P:(j + 1) * P], w2[:, u // HC, u % HC],
                                        start=(u == 0), stop=(u == U - 1))
                ins.then_inc(down_done, 1)

            over_chunks(pe, (0, widen), (1, narrow))

        @block.scalar
        def _(act):
            for turn in range(2):
                act.wait_ge(shifted, turn + 1)
                act.activation(ex[:], lg[:], ACT.Exp).then_inc(exp_done, 1)
            act.wait_ge(shifted, 3)
            act.activation(ex[:, 0:1], lg[:, 0:1], ACT.Exp).then_inc(exp_done, 1)
            act.wait_ge(experts_in, 128)

            def gelu(c, b, n):
                wait_past(act, down_done, c - 1)
                for u in range(U):
                    act.wait_ge(up_done, U * c + u + 1)
                    act.activation(hid[:, b, u], up[u % 4][:, 0:CHUNK], ACT.Gelu,
                                   bias=b1_sb[:, u // HC, u % HC:u % HC + 1]).then_inc(gelu_done, 1)

            over_chunks(act, (0, gelu))


def build(nc, a, out):
    emb = nc.dram_tensor("emb", [NODES_PAD, DIM], F32, kind="Internal").ap()
    emb_t = nc.dram_tensor("emb_t", [CHUNKS, P, DC * CHUNK], F32, kind="Internal").ap()
    h = nc.dram_tensor("h", [NODES_PAD, DIM], F32, kind="Internal").ap()
    h_t = nc.dram_tensor("h_t", [CHUNKS, P, DC * CHUNK], F32, kind="Internal").ap()
    x2 = nc.dram_tensor("x2", [NODES_PAD, DIM], F32, kind="Internal").ap()
    xl = nc.dram_tensor("xl", [NODES_PAD, DIM], F32, kind="Internal").ap()
    rel_kept = nc.dram_tensor("rel_kept", [GROUPS, P, GROUP, DIM], F32, kind="Internal").ap()
    with ExitStack() as ctx:
        K = {}

        def keep(name, shape, dt=F32):
            K[name] = ctx.enter_context(nc.sbuf_tensor(name, shape, dt))

        keep("ident", [P, P])
        keep("ones", [P, P])
        keep("minus_half", [P, 2])
        keep("eps", [P, 2])
        keep("zeros", [P, CHUNK, DC])
        keep("node_iota", [P, WIN])
        keep("res", [P, 1])
        keep("node_sums", [P, DC, CHUNKS])
        keep("acc", [P, 2 * ACC_W, DC])
        keep("deg", [P, ACC_W])
        with ExitStack() as edge_tables:
            for name, shape, dt in (("dst", [P, TILES], F32), ("dst_rel", [P, TILES], F32),
                                    ("base", [P, GROUPS], I32), ("acc_at", [P, GROUPS], I32),
                                    ("half_at", [P, GROUPS], I32), ("span", [P, 1], I32)):
                K[name] = edge_tables.enter_context(nc.sbuf_tensor(name, shape, dt))
            phase_setup(nc, K, a["x"], a["dst"], a["L0_gnn_res"], emb, emb_t)
            phase_edges(nc, K, 0, emb, a["rel"], a["src"], a["edge_type_400"], rel_kept)
            phase_dense(nc, K, 0, emb_t, h_t, h, a["L0_gnn_W_in1"], a["L0_gnn_W_out1"], a["L0_gnn_W_loop1"],
                        a["L0_gnn_b1"])
            phase_edges(nc, K, 1, h, None, a["src"], a["edge_type_400"], rel_kept)
        phase_dense(nc, K, 1, h_t, None, None, a["L0_gnn_W_in2"], a["L0_gnn_W_out2"], a["L0_gnn_W_loop2"],
                    a["L0_gnn_b2"], (a["x"], a["L0_gnn_mu_w"], a["L0_gnn_mu_b"], x2, xl))
        phase_ffn(nc, K, x2, xl, *(a["L0_ffn_" + n] for n in ("Wr", "br", "W1", "b1", "W2", "b2", "gamma", "beta")),
                  out)


def kernel(**inputs):
    import numpy as np
    from concourse import bacc
    from concourse.bass_utils import run_bass_kernel_spmd

    arrays = {n: np.ascontiguousarray(v) for n, v in inputs.items()}

    def by_tiles(v, fill):
        out = np.full((2, TILES_HALF * P), fill, v.dtype)
        out[:, :HALF] = v.reshape(2, HALF)
        return out.reshape(TILES, P)

    x = np.zeros((NODES_PAD, DIM), arrays["x"].dtype)
    x[:NODES] = arrays["x"]
    arrays["x"] = x
    for n in ("src", "edge_type_400"):
        blocks = by_tiles(arrays[n], 0).reshape(2 * STEPS, RING // 2, P)
        arrays[n] = np.ascontiguousarray(blocks.transpose(0, 2, 1))
    arrays["dst"] = np.ascontiguousarray(by_tiles(arrays["dst"], FAR).T)
    arrays["rel"] = np.concatenate([arrays.pop("L0_gnn_rel1"), arrays.pop("L0_gnn_rel2")], axis=1)

    nc = bacc.Bacc("TRN2", target_bir_lowering=False, num_devices=1)
    feeds, args = {}, {}
    for name, v in arrays.items():
        feeds[f"in_{name}"] = v
        args[name] = nc.dram_tensor(f"in_{name}", v.shape, mybir.dt.from_np(v.dtype), kind="ExternalInput").ap()
    out = nc.dram_tensor("out", [NODES_PAD, DIM], F32, kind="ExternalOutput").ap()
    build(nc, args, out)
    r = run_bass_kernel_spmd(nc, [feeds], core_ids=[0])
    return r.results[0]["out"][:NODES]
```

```python
from contextlib import ExitStack

import concourse.bass as bass
from concourse import mybir

ALU = mybir.AluOpType
ACT = mybir.ActivationFunctionType
F32 = mybir.dt.float32
I32 = mybir.dt.int32
U32 = mybir.dt.uint32
F32R = mybir.dt.float32r
AX_X = mybir.AxisListType.X
ds = bass.ds

P = 128
NODES, DIM = 6250, 256
DC = DIM // P
CHUNK = 2 * P
CHUNKS = -(-NODES // CHUNK)
NODES_PAD = CHUNKS * CHUNK
EDGES = 106250
HALF = EDGES // 2
GROUP = 4
RING = 16
GROUPS_IN_RING = RING // GROUP
TILES_HALF = -(-HALF // (P * RING)) * RING
TILES = 2 * TILES_HALF
GROUPS = TILES // GROUP
STEPS = TILES // RING
WIN = 64
HOT_ACT = 2
WINDOWS = -(-NODES // WIN)
ACC_W = NODES_PAD
assert NODES - 1 + WIN <= ACC_W
FAR = 16384
RELS = 400
FULL = RELS // P
REST = RELS - FULL * P
RCHUNKS = FULL + 1
assert 0 < REST and 2 * REST <= P
HID = 512
HC = HID // P
EXPERTS = 8
TOP = 2
EPS = 1e-5
BUFS = 4
CAPACITY = float(-(-NODES * 5 // (4 * EXPERTS)))


def wait_past(eng, sem, value):
    if not isinstance(value, int) or value > 0:
        eng.wait_ge(sem, value)


def wait_apart(eng, sem, value, passed):
    if not isinstance(value, int) or value > 0:
        eng.wait_ge(sem, value)
        eng.sem_inc(passed, 1)


def over_chunks(eng, *stages, ring=2):
    def turn(c, step, q):
        for lag, stage in stages:
            if not isinstance(c, int) or 0 <= c - lag < CHUNKS:
                stage(c - lag, (q - lag) % ring, step + (q - lag) // ring)

    last = max(lag for lag, _ in stages)
    assert last <= ring
    apart = 2 if last else 1
    for c in range(apart * ring):
        turn(c, c // ring, c % ring)
    with eng.Fori(apart, CHUNKS // ring) as i:
        for q in range(ring):
            turn(ring * i + q, i, q)
    for c in range(CHUNKS // ring * ring, CHUNKS + last):
        turn(c, c // ring, c % ring)


class Scope:

    def __init__(self, nc, ctx, name):
        self.nc, self.ctx, self.name = nc, ctx, name

    def sb(self, name, shape, dt=F32):
        return self.ctx.enter_context(self.nc.sbuf_tensor(f"{self.name}_{name}", shape, dt))

    def ps(self, name, shape, dt=F32):
        return self.ctx.enter_context(self.nc.psum_tensor(f"{self.name}_{name}", shape, dt))

    def sem(self, name):
        return self.ctx.enter_context(self.nc.semaphore(f"{self.name}_{name}"))


def rows_of(dram, c):
    return dram[ds(c * CHUNK, CHUNK), :].rearrange("(j p) d -> p j d", p=P)


def transposed(K, c, k):
    return K["acc"][:].rearrange("p n k -> p (n k)")[:, ds((c * DC + k) * CHUNK, CHUNK)]


def phase_setup(nc, K, x, dst_tiles, res, emb, emb_t):
    with ExitStack() as ctx:
        s = Scope(nc, ctx, "set")
        dst_i = s.sb("dst_i", [P, TILES], I32)
        neg = s.sb("neg", [P, TILES])
        real = s.sb("real", [P, TILES])
        neg_max = s.sb("neg_max", [P, TILES])
        real_max = s.sb("real_max", [P, TILES])
        gmin = s.sb("gmin", [P, GROUPS])
        gmax = s.sb("gmax", [P, GROUPS])
        half_at = s.sb("half_at", [P, GROUPS])
        acc_at = s.sb("acc_at", [P, GROUPS])
        span = s.sb("span", [P, GROUPS])
        span_max = s.sb("span_max", [P, 1])
        x_rows = s.sb("x_rows", [P, BUFS, 2, DIM])
        e_rows = s.sb("e_rows", [P, BUFS, 2, DIM])
        e_t = s.sb("e_t", [P, BUFS, DC, CHUNK])
        stats = s.sb("stats", [P, BUFS, 2, 6])
        mv = s.sb("mv", [P, BUFS, 2, 2])
        rstd = s.sb("rstd", [P, BUFS, 2])
        tr = [s.ps(f"tr{b}", [P, DC, CHUNK]) for b in range(BUFS)]

        dst_in = s.sem("dst_in")
        res_in = s.sem("res_in")
        consts = s.sem("consts")
        zeroed = s.sem("zeroed")
        chain = s.sem("chain")
        reduced = s.sem("reduced")
        x_in = [s.sem(f"x_in{b}") for b in range(BUFS)]
        stats_done = s.sem("stats_done")
        mv_done = s.sem("mv_done")
        rstd_half = s.sem("rstd_half")
        rstd_done = s.sem("rstd_done")
        emb_done = s.sem("emb_done")
        tr_done = s.sem("tr_done")
        copied = s.sem("copied")
        stored = [s.sem(f"stored{b}") for b in range(BUFS)]
        passed = s.sem("passed")
        block = ctx.enter_context(nc.Block())

        @block.sync
        def _(sp):
            sp.dma_start(dst_i[:], dst_tiles).then_inc(dst_in, 16)
            sp.dma_start(K["res"][:], res.partition_broadcast(P)).then_inc(res_in, 16)

            def load(c, b, n):
                wait_past(sp, emb_done, c + 1 - BUFS)
                sp.dma_start(x_rows[:, b], rows_of(x, c)).then_inc(x_in[b], 16)

            def store(c, b, n):
                sp.wait_ge(emb_done, c + 1)
                sp.dma_start(rows_of(emb, c), e_rows[:, b]).then_inc(stored[b], 16)
                sp.wait_ge(copied, c + 1)
                sp.dma_start(emb_t[ds(c, 1)].rearrange("o p f -> p (o f)"),
                             e_t[:, b].rearrange("p k n -> p (k n)")).then_inc(stored[b], 16)

            over_chunks(sp, (0, load), (3, store), ring=BUFS)
            sp.wait_ge(res_in, 16)
            for b in range(BUFS):
                sp.wait_ge(stored[b], 32 * -(-(CHUNKS - b) // BUFS))

        @block.gpsimd
        def _(pool):
            pool.memset(K["ident"][:], 0.0).then_inc(consts, 1)
            pool.memset(K["ones_r"][:].bitcast(F32), 1.0).then_inc(consts, 1)
            pool.iota(K["type_of"][:], [[P, RCHUNKS]], base=0, channel_multiplier=1,
                      allow_small_or_imprecise_dtypes=True).then_inc(consts, 1)
            pool.memset(K["minus_half"][:], -0.5).then_inc(consts, 1)
            pool.memset(K["eps"][:], EPS).then_inc(consts, 1)
            pool.memset(K["zeros"][:], 0.0).then_inc(consts, 1)
            pool.iota(K["node_iota"][:], [[1, WIN]], base=0, channel_multiplier=0,
                      allow_small_or_imprecise_dtypes=True).then_inc(consts, 1)
            pool.iota(half_at[:], [[ACC_W, 2], [0, GROUPS // 2]], base=0, channel_multiplier=0,
                      allow_small_or_imprecise_dtypes=True).then_inc(consts, 1)
            pool.wait_ge(consts, 8)
            pool.affine_select(out=K["ident"][:], in_=K["ident"][:], compare_op=ALU.not_equal, fill=1.0,
                               base=0, pattern=[[-1, P]], channel_multiplier=1).then_inc(consts, 1)

            def inverse_deviation(c, b, n):
                pool.wait_ge(mv_done, 2 * c + 2)
                wait_past(pool, emb_done, c + 1 - BUFS)
                pool.tensor_tensor(rstd[:, b], mv[:, b, :, 1], K["eps"][:], ALU.add).then_inc(rstd_half, 1)
                pool.wait_ge(rstd_half, c + 1)
                pool.tensor_tensor(rstd[:, b], rstd[:, b], K["minus_half"][:, 0:2], ALU.pow).then_inc(rstd_done, 1)

            over_chunks(pool, (0, inverse_deviation), ring=BUFS)
            pool.wait_ge(chain, 3)
            pool.partition_all_reduce(neg_max[:], neg[:], P, bass.bass_isa.ReduceOp.max).then_inc(reduced, 1)
            pool.partition_all_reduce(real_max[:], real[:], P, bass.bass_isa.ReduceOp.max).then_inc(reduced, 1)

        @block.vector
        def _(dve):
            dve.wait_ge(dst_in, 16)
            dve.tensor_copy(K["dst"][:], dst_i[:]).then_inc(chain, 1)
            dve.wait_ge(chain, 1)
            dve.tensor_scalar(neg[:], K["dst"][:], -1.0, None, ALU.mult).then_inc(chain, 1)
            dve.scalar_tensor_tensor(real[:], K["dst"][:], float(FAR), K["dst"][:],
                                     ALU.is_lt, ALU.mult).then_inc(chain, 1)

            def moments(c, b, n):
                dve.wait_ge(x_in[b], 16 * (n + 1))
                for j in range(2):
                    dve.bn_stats(stats[:, b, j], x_rows[:, b, j]).then_inc(stats_done, 1)
                wait_past(dve, emb_done, c + 1 - BUFS)
                for j in range(2):
                    wait_apart(dve, stats_done, 2 * c + 1 + j, passed)
                    dve.bn_aggr(mv[:, b, j], stats[:, b, j]).then_inc(mv_done, 1)

            def normalize(c, b, n):
                dve.wait_ge(rstd_done, c + 1)
                wait_past(dve, stored[b], 32 * n)
                wait_past(dve, tr_done, c + 1 - BUFS)
                for j in range(2):
                    ins = dve.tensor_scalar(e_rows[:, b, j], x_rows[:, b, j], mv[:, b, j, 0:1],
                                            rstd[:, b, j:j + 1], ALU.subtract, ALU.mult)
                ins.then_inc(emb_done, 1)

            over_chunks(dve, (0, moments), (1, normalize), ring=BUFS)

            dve.wait_ge(reduced, 2)
            dve.wait_ge(consts, 9)
            dve.tensor_reduce(gmin[:], neg_max[:].rearrange("p (g t) -> p g t", t=GROUP), AX_X,
                              ALU.max).then_inc(chain, 1)
            dve.tensor_reduce(gmax[:], real_max[:].rearrange("p (g t) -> p g t", t=GROUP), AX_X,
                              ALU.max).then_inc(chain, 1)
            dve.wait_ge(chain, 5)
            dve.tensor_tensor(span[:], gmax[:], gmin[:], ALU.add).then_inc(chain, 1)
            dve.tensor_tensor(K["dst_rel"][:].rearrange("p (g t) -> p g t", t=GROUP),
                              K["dst"][:].rearrange("p (g t) -> p g t", t=GROUP),
                              gmin[:].unsqueeze(2).to_broadcast([P, GROUPS, GROUP]), ALU.add).then_inc(chain, 1)
            dve.tensor_scalar(K["base"][:], gmin[:], -1.0, None, ALU.mult).then_inc(chain, 1)
            dve.tensor_tensor(acc_at[:], half_at[:], gmin[:], ALU.subtract).then_inc(chain, 1)
            dve.tensor_copy(K["half_at"][:], half_at[:]).then_inc(chain, 1)
            dve.wait_ge(chain, 10)
            dve.tensor_copy(K["acc_at"][:], acc_at[:]).then_inc(chain, 1)
            dve.tensor_reduce(span_max[:], span[:], AX_X, ALU.max).then_inc(chain, 1)
            dve.wait_ge(chain, 12)
            dve.tensor_copy(K["span"][:], span_max[:]).then_inc(chain, 1)
            dve.tensor_scalar(K["type_of"][32:64, FULL:], K["type_of"][32:64, FULL:], -32.0, None,
                              ALU.add).then_inc(chain, 1)
            dve.wait_ge(chain, 14)
            dve.tensor_scalar(K["minus_type"][:], K["type_of"][:], -1.0, None, ALU.mult).then_inc(chain, 1)

        @block.tensor
        def _(pe):
            pe.wait_ge(consts, 9)

            def transpose(c, b, n):
                pe.wait_ge(emb_done, c + 1)
                wait_past(pe, copied, c + 1 - BUFS)
                for k in range(DC):
                    for j in range(2):
                        ins = pe.transpose(tr[b][:, k, j * P:(j + 1) * P],
                                           e_rows[:, b, j, k * P:(k + 1) * P], K["ident"][:])
                ins.then_inc(tr_done, 1)

            over_chunks(pe, (0, transpose), ring=BUFS)

        @block.scalar
        def _(act):
            def copy(c, b, n):
                act.wait_ge(tr_done, c + 1)
                wait_past(act, stored[b], 32 * n)
                act.copy(e_t[:, b], tr[b][:]).then_inc(copied, 1)

            def clear(c, b, n):
                for h in range(2):
                    act.copy(K["acc"][:, ds(h * ACC_W + c * CHUNK, CHUNK), :], K["zeros"][:]).then_inc(zeroed, 1)
                act.copy(K["deg"][:, ds(c * CHUNK, CHUNK)], K["zeros"][:, :, 0]).then_inc(zeroed, 1)

            act.wait_ge(consts, 8)
            over_chunks(act, (0, copy), (0, clear), ring=BUFS)


def over_groups(eng, *stages):
    def turn(i, q):
        for lag, stage in stages:
            step = i + (q - lag) // GROUPS_IN_RING
            g = GROUPS_IN_RING * i + q - lag
            if not isinstance(g, int) or 0 <= g < GROUPS:
                stage(g, (q - lag) % GROUPS_IN_RING, step)

    for i in range(2):
        for q in range(GROUPS_IN_RING):
            turn(i, q)
    with eng.Fori(2, STEPS) as i:
        for q in range(GROUPS_IN_RING):
            turn(i, q)
    for t in range(max(lag for lag, _ in stages)):
        turn(STEPS + t // GROUPS_IN_RING, t % GROUPS_IN_RING)


def phase_edges(nc, K, layer, nodes, rel, src_idx, types):
    first = layer == 0
    with ExitStack() as ctx:
        s = Scope(nc, ctx, f"edge{layer}")
        rel_hi = s.sb("rel_hi", [P, RCHUNKS, DIM], F32R)
        rel_lo = s.sb("rel_lo", [P, FULL, DIM], F32R)
        typ = s.sb("typ", [P, 2, GROUP * P], I32)
        hot = s.sb("hot", [P, 2, RCHUNKS, GROUP * P], F32R)
        xg = s.sb("xg", [P, RING, DIM])
        rel_sb = xg[:, RING - RCHUNKS:RING, :]
        m_hi = s.sb("m_hi", [P, 2, GROUP, DIM + 2], F32R)
        m_lo = s.sb("m_lo", [P, 2, GROUP, DIM], F32R)
        sel = s.sb("sel", [P, RING, P], F32R)
        sums_sb = s.sb("sums_sb", [WIN, 2, DIM + 2])
        src_i = s.sb("src_i", [P, 2, RING // 2], I32)
        shifted = s.sb("shifted", [P, GROUP])
        win_base = s.sb("win_base", [P, 1])
        rg = [s.ps(f"rg{b}", [P, GROUP, DIM]) for b in range(2)]
        sums = [s.ps(f"sums{b}", [P, DIM + 2]) for b in range(2)]
        sums_t = [s.ps(f"sums_t{b}", [P, DC + 1, WIN]) for b in range(2)]

        rel_zero = s.sem("rel_zero")
        rel_in = s.sem("rel_in")
        rel_split = s.sem("rel_split")
        src_in = [s.sem(f"src_in{b}") for b in range(2)]
        typ_in = [s.sem(f"typ_in{b}") for b in range(2)]
        gathered = [s.sem(f"gathered{q}") for q in range(GROUPS_IN_RING)]
        hot_done = s.sem("hot_done")
        distances = s.sem("distances")
        hot_act = s.sem("hot_act")
        rel_done = s.sem("rel_done")
        selected = s.sem("selected")
        messages = s.sem("messages")
        hi_done = s.sem("hi_done")
        lo_done = s.sem("lo_done")
        filled = s.sem("filled")
        summed = s.sem("summed")
        sums_copied = s.sem("sums_copied")
        turned = s.sem("turned")
        acc_added = s.sem("acc_added")
        deg_added = s.sem("deg_added")
        win_step = s.sem("win_step")
        win_selected = s.sem("win_selected")
        win_summed = s.sem("win_summed")
        win_added = s.sem("win_added")
        win_deg = s.sem("win_deg")
        passed = s.sem("passed")
        block = ctx.enter_context(nc.Block())

        @block.sync
        def _(sp):
            sp.dma_start(rel_sb[:, 0:FULL, :], rel[0:FULL * P, :].rearrange("(c p) d -> p c d", p=P))\
              .then_inc(rel_in, 16)
            sp.wait_ge(rel_zero, 1)
            for at in (0, 32):
                sp.dma_start(rel_sb[at:at + REST, FULL, :], rel[FULL * P:RELS, :]).then_inc(rel_in, 16)

            def load(g, q, i):
                if q % 2 == 0:
                    for k in (q, q + 1):
                        wait_past(sp, gathered[k], 16 * GROUP * i)
                    sp.dma_start(src_i[:, q // 2], src_idx[ds(2 * i + q // 2, 1)].rearrange("o p k -> p (o k)"))\
                      .then_inc(src_in[q // 2], 16)
                wait_past(sp, hot_done, g - 1)
                wait_past(sp, hot_act, g - 1)
                sp.dma_start(typ[:, q % 2], types[ds(g * GROUP * P, GROUP * P)].partition_broadcast(P))\
                  .then_inc(typ_in[q % 2], 16)

            over_groups(sp, (0, load))

        @block.gpsimd
        def _(pool):
            def gather(g, q, i):
                if isinstance(g, int) and g == GROUPS_IN_RING - 1:
                    pool.wait_ge(rel_split, 3)
                wait_apart(pool, lo_done, g + 1 - GROUPS_IN_RING, passed)
                if q % 2 == 0:
                    wait_apart(pool, src_in[q // 2], 16 * (i + 1), passed)
                for t in range(GROUP * q, GROUP * (q + 1)):
                    at = src_i[:, t // (RING // 2), t % (RING // 2):t % (RING // 2) + 1]
                    pool.indirect_dma_start(xg[:, t, :], None, nodes,
                                            bass.IndirectOffsetOnAxis(ap=at, axis=0)).then_inc(gathered[q], 16)

            over_groups(pool, (0, gather))

        @block.scalar
        def _(act):
            def high(g, q, i):
                act.wait_ge(messages, g + 1)
                wait_past(act, summed, g - 1)
                act.copy(m_hi[:, q % 2, :, 0:DIM], xg[:, GROUP * q:GROUP * (q + 1), :]).then_inc(hi_done, 1)

            def one_hot(g, q, i):
                act.wait_ge(typ_in[q % 2], 16 * ((2 * i + q // 2) + 1))
                wait_past(act, rel_done, g - 1)
                for c in range(HOT_ACT):
                    act.activation(hot[:, q % 2, c], typ[:, q % 2], ACT.Abs,
                                   bias=K["minus_type"][:, c:c + 1]).then_inc(distances, 1)
                for c in range(HOT_ACT):
                    act.wait_ge(distances, HOT_ACT * g + c + 1)
                    ins = act.activation(hot[:, q % 2, c], hot[:, q % 2, c].bitcast(F32), ACT.Relu,
                                         bias=1.0, scale=-1.0)
                ins.then_inc(hot_act, 1)

            def copy_sums(g, q, i):
                act.wait_ge(summed, g + 1)
                wait_past(act, turned, g - 1)
                act.copy(sums_sb[:, q % 2], sums[q % 2][0:WIN, :]).then_inc(sums_copied, 1)

            widest = act.value_load(K["span"][0:1, 0:1], min_val=0, max_val=2 * FAR)
            with act.If(widest < WIN):
                over_groups(act, (4, copy_sums), (0, one_hot), (2, high))
            with act.Else():
                over_groups(act, (0, one_hot), (2, high))

        @block.vector
        def _(dve):
            dve.memset(sel[:].bitcast(F32), 0.0).then_inc(filled, 1)
            dve.memset(m_hi[:, :, :, DIM:].bitcast(F32), 0.0).then_inc(filled, 1)
            dve.wait_ge(filled, 2)
            dve.memset(m_hi[:, :, :, DIM:DIM + 1].bitcast(F32), 1.0).then_inc(filled, 1)
            dve.memset(rel_sb[:, FULL, :], 0.0).then_inc(rel_zero, 1)
            dve.wait_ge(rel_in, 48)
            dve.tensor_copy(rel_hi[:], rel_sb).then_inc(rel_split, 1)
            dve.wait_ge(rel_split, 1)
            dve.tensor_tensor(rel_lo[:], rel_sb[:, 0:FULL, :], rel_hi[:, 0:FULL, :].bitcast(F32),
                              ALU.subtract).then_inc(rel_split, 1)
            dve.tensor_tensor(rel_hi[32:32 + REST, FULL, :], rel_sb[32:32 + REST, FULL, :],
                              rel_hi[32:32 + REST, FULL, :].bitcast(F32), ALU.subtract).then_inc(rel_split, 1)

            def one_hot(g, q, i):
                dve.wait_ge(typ_in[q % 2], 16 * ((2 * i + q // 2) + 1))
                wait_past(dve, rel_done, g - 1)
                for c in range(HOT_ACT, RCHUNKS):
                    ins = dve.tensor_scalar(hot[:, q % 2, c], typ[:, q % 2], K["type_of"][:, c:c + 1], None,
                                            ALU.is_equal)
                ins.then_inc(hot_done, 1)

            def message(g, q, i):
                at = slice(GROUP * q, GROUP * (q + 1))
                dve.wait_ge(gathered[q], 16 * GROUP * (i + 1))
                dve.wait_ge(rel_done, g + 1)
                dve.tensor_tensor(xg[:, at, :], xg[:, at, :], rg[q % 2][:], ALU.mult).then_inc(messages, 1)

            def low(g, q, i):
                dve.wait_ge(hi_done, g + 1)
                wait_past(dve, summed, g - 1)
                dve.tensor_tensor(m_lo[:, q % 2], xg[:, GROUP * q:GROUP * (q + 1), :],
                                  m_hi[:, q % 2, :, 0:DIM].bitcast(F32),
                                  ALU.subtract).then_inc(lo_done, 1)

            def select(out, dst):
                return dve.tensor_tensor(out, K["node_iota"][:].unsqueeze(1).to_broadcast([P, GROUP, WIN]),
                                         dst.unsqueeze(2).to_broadcast([P, GROUP, WIN]), ALU.is_equal)

            def add(b, base, acc_at, added, counted):
                part = K["acc"][:, ds(acc_at, WIN), :]
                dve.tensor_tensor(part, part, sums_t[b][:, 0:DC, :].rearrange("p k n -> p n k"),
                                  ALU.add).then_inc(added, 1)
                if first:
                    part = K["deg"][:, ds(base, WIN)]
                    dve.tensor_tensor(part, part, sums_t[b][:, DC, :], ALU.add).then_inc(counted, 1)

            def short():
                def one_window(g, q, i):
                    wait_past(dve, summed, g + 1 - GROUPS_IN_RING)
                    select(sel[:, GROUP * q:GROUP * (q + 1), 0:WIN],
                           K["dst_rel"][:, ds(GROUP * g, GROUP)]).then_inc(selected, 1)

                def add_window(g, q, i):
                    base = dve.value_load(K["base"][0:1, ds(g, 1)], min_val=0, max_val=ACC_W - WIN) if first else None
                    acc_at = dve.value_load(K["acc_at"][0:1, ds(g, 1)], min_val=0, max_val=2 * ACC_W - WIN)
                    dve.wait_ge(turned, g + 1)
                    wait_past(dve, acc_added, g)
                    if first:
                        wait_past(dve, deg_added, g)
                    add(q % 2, base, acc_at, acc_added, deg_added)

                over_groups(dve, (0, one_hot), (1, one_window), (2, message), (5, add_window), (3, low))

            def long():
                dve.sem_inc(win_added, 1)
                if first:
                    dve.sem_inc(win_deg, 1)

                def all_windows(g, q, i):
                    half_at = dve.value_load(K["half_at"][0:1, ds(g, 1)], min_val=0, max_val=ACC_W)
                    dve.memset(win_base[:], -float(WIN)).then_inc(win_step, 1)
                    with dve.Fori(0, WINDOWS) as w:
                        dve.wait_ge(win_step, g * (2 * WINDOWS + 1) + 2 * w + 1)
                        dve.tensor_scalar(win_base[:], win_base[:], float(WIN), None, ALU.add).then_inc(win_step, 1)
                        dve.wait_ge(win_step, g * (2 * WINDOWS + 1) + 2 * w + 2)
                        dve.tensor_scalar(shifted[:], K["dst"][:, ds(GROUP * g, GROUP)], win_base[:, 0:1], None,
                                          ALU.subtract).then_inc(win_step, 1)
                        dve.wait_ge(win_step, g * (2 * WINDOWS + 1) + 2 * w + 3)
                        select(sel[:, GROUP * q:GROUP * (q + 1), 0:WIN], shifted[:]).then_inc(win_selected, 1)
                        dve.wait_ge(win_summed, g * WINDOWS + w + 1)
                        add(0, w * WIN, half_at + w * WIN, win_added, win_deg)

                over_groups(dve, (0, one_hot), (2, message), (3, low), (3, all_windows))
                dve.wait_ge(win_added, GROUPS * WINDOWS + 1)

            widest = dve.value_load(K["span"][0:1, 0:1], min_val=0, max_val=2 * FAR)
            with dve.If(widest < WIN):
                short()
            with dve.Else():
                long()

        @block.tensor
        def _(pe):
            pe.wait_ge(rel_split, 3)
            pe.wait_ge(filled, 3)

            def relation_rows(g, q, i):
                pe.wait_ge(hot_done, g + 1)
                pe.wait_ge(hot_act, g + 1)
                wait_past(pe, messages, g - 1)
                for t in range(GROUP):
                    for c in range(RCHUNKS):
                        for part in (rel_hi, rel_lo) if c < FULL else (rel_hi,):
                            ins = pe.matmul(rg[q % 2][:, t, :], hot[:, q % 2, c, t * P:(t + 1) * P], part[:, c, :],
                                            start=(c == 0 and part is rel_hi), stop=(c == FULL))
                ins.then_inc(rel_done, 1)

            def short():
                def one_window(g, q, i):
                    pe.wait_ge(selected, g + 1)
                    pe.wait_ge(lo_done, g + 1)
                    wait_past(pe, sums_copied, g - 1)
                    for t in range(GROUP):
                        lhs = sel[:, GROUP * q + t, :]
                        pe.matmul(sums[q % 2][:], lhs, m_hi[:, q % 2, t, :], start=(t == 0), stop=False)
                        ins = pe.matmul(sums[q % 2][:, 0:DIM], lhs, m_lo[:, q % 2, t, :], start=False,
                                        stop=(t == GROUP - 1))
                    ins.then_inc(summed, 1)

                def turn_over(g, q, i):
                    pe.wait_ge(sums_copied, g + 1)
                    if first:
                        wait_past(pe, deg_added, g - 1)
                    wait_apart(pe, acc_added, g - 1, passed)
                    for k in range(DC):
                        ins = pe.transpose(sums_t[q % 2][:, k, :], sums_sb[:, q % 2, k * P:(k + 1) * P],
                                           K["ident"][0:WIN, 0:WIN])
                    if first:
                        ins = pe.transpose(sums_t[q % 2][:, DC, :],
                                           sums_sb[:, q % 2, DIM:DIM + 1].to_broadcast([WIN, P]),
                                           K["ident"][0:WIN, 0:WIN])
                    ins.then_inc(turned, 1)

                over_groups(pe, (1, relation_rows), (3, one_window), (4, turn_over))

            def long():
                def sum_window(q):
                    for k in range(DC):
                        for part in (m_hi, m_lo):
                            for t in range(GROUP):
                                ins = pe.matmul(sums_t[0][:, k, :], part[:, q % 2, t, k * P:(k + 1) * P],
                                                sel[:, GROUP * q + t, 0:WIN], start=(part is m_hi and t == 0),
                                                stop=(part is m_lo and t == GROUP - 1))
                    if first:
                        for t in range(GROUP):
                            ins = pe.matmul(sums_t[0][:, DC, :], K["ones_r"][:], sel[:, GROUP * q + t, 0:WIN],
                                            start=(t == 0), stop=(t == GROUP - 1))
                    return ins

                def all_windows(g, q, i):
                    wait_apart(pe, lo_done, g + 1, passed)
                    with pe.Fori(0, WINDOWS) as w:
                        pe.wait_ge(win_selected, g * WINDOWS + w + 1)
                        pe.wait_ge(win_added, g * WINDOWS + w + 1)
                        if first:
                            pe.wait_ge(win_deg, g * WINDOWS + w + 1)
                        sum_window(q).then_inc(win_summed, 1)
                    pe.wait_ge(win_added, (g + 1) * WINDOWS + 1)
                    pe.sem_inc(summed, 1)

                over_groups(pe, (1, relation_rows), (3, all_windows))

            widest = pe.value_load(K["span"][0:1, 0:1], min_val=0, max_val=2 * FAR)
            with pe.If(widest < WIN):
                short()
            with pe.Else():
                long()


def phase_dense(nc, K, layer, prev_t, next_t, next_rows, W_in, W_out, W_loop, b, tail=None):
    first = layer == 0
    with ExitStack() as ctx:
        s = Scope(nc, ctx, f"dense{layer}")
        w_sb = s.sb("w", [P, 3, DC, DIM])
        b_sb = s.sb("b", [P, DC])
        prev = s.sb("prev", [P, 2, DC, CHUNK])
        scaled = s.sb("scaled", [P, 2, 2, DC, CHUNK])
        th = s.sb("th", [P, 2, DC, CHUNK])
        h_t = s.sb("h_t", [P, 2, DC, CHUNK])
        lin = [s.ps(f"lin{k}", [P, DC, CHUNK]) for k in range(2)]
        tr = [s.ps(f"tr{k}", [P, 2, DIM]) for k in range(2)]
        rows = s.sb("rows", [P, 2, 2, DIM])

        w_in = s.sem("w_in")
        prev_in = [s.sem(f"prev_in{k}") for k in range(2)]
        clamped = s.sem("clamped")
        normed = s.sem("normed")
        scaled_done = s.sem("scaled_done")
        cleared = s.sem("cleared")
        lin_done = s.sem("lin_done")
        tanh_done = s.sem("tanh_done")
        h_done = s.sem("h_done")
        tr_done = s.sem("tr_done")
        rows_done = s.sem("rows_done")
        rows_out = [s.sem(f"rows_out{k}") for k in range(2)]
        t_out = [s.sem(f"t_out{k}") for k in range(2)]
        if not first:
            x, mu_w, mu_b, x2_dram, xl_dram = tail
            mu_sb = s.sb("mu_w", [P, DC, DIM])
            mub_sb = s.sb("mu_b", [P, DIM])
            xb = s.sb("xb", [P, 2, 2, DIM])
            x2 = s.sb("x2", [P, 2, 2, DIM])
            stats = s.sb("stats", [P, 2, 2, 6])
            mv = s.sb("mv", [P, 2, 2, 2])
            rstd = s.sb("rstd", [P, 2, 2])
            mu = [s.ps(f"mu{k}", [P, 2, DIM]) for k in range(2)]
            x_in = [s.sem(f"x_in{k}") for k in range(2)]
            xb_done = s.sem("xb_done")
            mu_done = s.sem("mu_done")
            x2_done = s.sem("x2_done")
            stats_done = s.sem("stats_done")
            mv_done = s.sem("mv_done")
            rstd_half = s.sem("rstd_half")
            rstd_done = s.sem("rstd_done")
            cols_done = s.sem("cols_done")
            x2_out = [s.sem(f"x2_out{k}") for k in range(2)]
        n_w = 3 + 1 + (0 if first else 2)
        passed = s.sem("passed")
        block = ctx.enter_context(nc.Block())

        @block.sync
        def _(sp):
            for k, w in enumerate((W_in, W_out, W_loop)):
                sp.dma_start(w_sb[:, k], w.rearrange("(c p) m -> p c m", p=P)).then_inc(w_in, 16)
            sp.dma_start(b_sb[:], b.rearrange("(c p) -> p c", p=P),
                         allow_slow_non_contiguous=True).then_inc(w_in, 16)
            if not first:
                sp.dma_start(mu_sb[:], mu_w.rearrange("(c p) m -> p c m", p=P)).then_inc(w_in, 16)
                sp.dma_start(mub_sb[:], mu_b.partition_broadcast(P)).then_inc(w_in, 16)

            def load(c, b, n):
                wait_past(sp, h_done, c - 1)
                sp.dma_start(prev[:, b].rearrange("p k n -> p (k n)"),
                             prev_t[ds(c, 1)].rearrange("o p f -> p (o f)")).then_inc(prev_in[b], 16)
                if not first:
                    wait_past(sp, x2_done, c - 1)
                    sp.dma_start(xb[:, b], rows_of(x, c)).then_inc(x_in[b], 16)

            def store_t(c, b, n):
                sp.wait_ge(h_done, c + 1)
                sp.dma_start(next_t[ds(c, 1)].rearrange("o p f -> p (o f)"),
                             h_t[:, b].rearrange("p k n -> p (k n)")).then_inc(t_out[b], 16)

            def store_rows(c, b, n):
                sp.wait_ge(rows_done, c + 1)
                sp.dma_start(rows_of(next_rows, c), rows[:, b]).then_inc(rows_out[b], 16)

            def store_x2(c, b, n):
                sp.wait_ge(x2_done, c + 1)
                sp.dma_start(rows_of(x2_dram, c), x2[:, b]).then_inc(x2_out[b], 16)
                sp.wait_ge(rows_done, c + 1)
                sp.dma_start(rows_of(xl_dram, c), rows[:, b]).then_inc(rows_out[b], 16)

            if first:
                over_chunks(sp, (0, load), (1, store_t), (2, store_rows))
            else:
                over_chunks(sp, (0, load), (2, store_x2))
            for k in range(2):
                times = (CHUNKS + 1 - k) // 2
                sp.wait_ge(rows_out[k], 16 * times)
                sp.wait_ge(t_out[k] if first else x2_out[k], 16 * times)

        @block.gpsimd
        def _(pool):
            if first:
                def clear(c, b, n):
                    pool.wait_ge(scaled_done, 2 * c + 2)
                    for h in range(2):
                        pool.tensor_copy(K["acc"][:, ds(h * ACC_W + c * CHUNK, CHUNK), :], K["zeros"][:]).then_inc(cleared, 1)

                over_chunks(pool, (0, clear))
                return
            pool.wait_ge(w_in, 16 * n_w)

            def add_bias(c, b, n):
                pool.wait_ge(x_in[b], 16 * (n + 1))
                pool.tensor_tensor(xb[:, b], xb[:, b], mub_sb[:].unsqueeze(1).to_broadcast([P, 2, DIM]),
                                   ALU.add).then_inc(xb_done, 1)

            def inverse_deviation(c, b, n):
                pool.wait_ge(mv_done, 2 * c + 2)
                wait_past(pool, rows_done, c - 1)
                pool.tensor_tensor(rstd[:, b], mv[:, b, :, 1], K["eps"][:], ALU.add).then_inc(rstd_half, 1)
                pool.wait_ge(rstd_half, c + 1)
                pool.tensor_tensor(rstd[:, b], rstd[:, b], K["minus_half"][:, 0:2], ALU.pow).then_inc(rstd_done, 1)

            over_chunks(pool, (0, add_bias), (2, inverse_deviation))

        @block.vector
        def _(dve):
            def scale(c, b, n):
                norm = K["deg"][:, ds(c * CHUNK, CHUNK)]
                if first:
                    dve.tensor_scalar(norm, norm, 1.0, None, ALU.max).then_inc(clamped, 1)
                    wait_apart(dve, clamped, c + 1, passed)
                    dve.reciprocal(norm, norm).then_inc(normed, 1)
                    dve.wait_ge(normed, c + 1)
                wait_past(dve, lin_done, c - 1)
                for h in range(2):
                    dve.tensor_tensor(
                        scaled[:, b, h],
                        K["acc"][:, ds(h * ACC_W + c * CHUNK, CHUNK), :].rearrange("p n k -> p k n"),
                        norm.unsqueeze(1).to_broadcast([P, DC, CHUNK]), ALU.mult).then_inc(scaled_done, 1)

            def residual(c, b, n):
                dve.wait_ge(tanh_done, 2 * c + 2)
                if first:
                    wait_past(dve, tr_done, c - 1)
                    wait_past(dve, t_out[b], 16 * n)
                else:
                    wait_past(dve, mu_done, c - 1)
                dve.scalar_tensor_tensor(h_t[:, b], th[:, b], K["res"][:, 0:1], prev[:, b], ALU.mult,
                                         ALU.add).then_inc(h_done, 1)

            def second_norm(c, b, n):
                dve.wait_ge(mu_done, c + 1)
                dve.wait_ge(xb_done, c + 1)
                wait_past(dve, x2_out[b], 16 * n)
                dve.tensor_tensor(x2[:, b], xb[:, b], mu[b][:], ALU.add).then_inc(x2_done, 1)
                dve.wait_ge(x2_done, c + 1)
                for j in range(2):
                    dve.bn_stats(stats[:, b, j], x2[:, b, j]).then_inc(stats_done, 1)
                for j in range(2):
                    wait_apart(dve, stats_done, 2 * c + 1 + j, passed)
                    dve.bn_aggr(mv[:, b, j], stats[:, b, j]).then_inc(mv_done, 1)
                dve.wait_ge(rstd_done, c + 1)
                wait_past(dve, tr_done, c - 1)
                wait_past(dve, rows_out[b], 16 * n)
                for j in range(2):
                    ins = dve.tensor_scalar(rows[:, b, j], x2[:, b, j], mv[:, b, j, 0:1], rstd[:, b, j:j + 1],
                                            ALU.subtract, ALU.mult)
                ins.then_inc(rows_done, 1)

            dve.wait_ge(w_in, 16 * n_w)
            if first:
                over_chunks(dve, (0, scale), (1, residual))
            else:
                over_chunks(dve, (0, scale), (1, residual), (2, second_norm))

        @block.tensor
        def _(pe):
            pe.wait_ge(w_in, 16 * n_w)

            def linear(c, b, n):
                pe.wait_ge(prev_in[b], 16 * (n + 1))
                pe.wait_ge(scaled_done, 2 * c + 2)
                wait_past(pe, tanh_done, 2 * c - 2)
                for m in range(DC):
                    cols = slice(m * P, (m + 1) * P)
                    for k in range(DC):
                        pe.matmul(lin[b][:, m, :], w_sb[:, 2, k, cols], prev[:, b, k], start=(k == 0), stop=False)
                    for h in range(2):
                        for k in range(DC):
                            ins = pe.matmul(lin[b][:, m, :], w_sb[:, h, k, cols], scaled[:, b, h, k],
                                            start=False, stop=(h == 1 and k == DC - 1))
                ins.then_inc(lin_done, 1)

            def to_rows(c, b, n):
                pe.wait_ge(h_done, c + 1)
                wait_past(pe, rows_done, c - 1)
                for j in range(2):
                    for k in range(DC):
                        ins = pe.transpose(tr[b][:, j, k * P:(k + 1) * P], h_t[:, b, k, j * P:(j + 1) * P],
                                           K["ident"][:])
                ins.then_inc(tr_done, 1)

            def project(c, b, n):
                pe.wait_ge(h_done, c + 1)
                wait_past(pe, x2_done, c - 1)
                for j in range(2):
                    for k in range(DC):
                        ins = pe.matmul(mu[b][:, j, :], h_t[:, b, k, j * P:(j + 1) * P], mu_sb[:, k, :],
                                        start=(k == 0), stop=(k == DC - 1))
                ins.then_inc(mu_done, 1)

            def to_columns(c, b, n):
                pe.wait_ge(rows_done, c + 1)
                wait_past(pe, cols_done, 2 * c - 2)
                for k in range(DC):
                    for j in range(2):
                        ins = pe.transpose(tr[b][:, k, j * P:(j + 1) * P], rows[:, b, j, k * P:(k + 1) * P],
                                           K["ident"][:])
                ins.then_inc(tr_done, 1)

            if first:
                over_chunks(pe, (0, linear), (1, to_rows))
            else:
                over_chunks(pe, (0, linear), (1, project), (2, to_columns))

        @block.scalar
        def _(act):
            act.wait_ge(w_in, 16 * n_w)

            def tanh(c, b, n):
                act.wait_ge(lin_done, c + 1)
                wait_past(act, h_done, c - 1)
                for m in range(DC):
                    act.activation(th[:, b, m], lin[b][:, m, :], ACT.Tanh, bias=b_sb[:, m:m + 1]).then_inc(tanh_done, 1)

            def copy_rows(c, b, n):
                act.wait_ge(tr_done, c + 1)
                wait_past(act, rows_out[b], 16 * n)
                act.copy(rows[:, b], tr[b][:]).then_inc(rows_done, 1)

            def copy_columns(c, b, n):
                act.wait_ge(tr_done, c + 1)
                whole = not isinstance(c, int) or (c + 1) * CHUNK <= NODES
                real = CHUNK if whole else NODES - c * CHUNK
                for k in range(DC):
                    act.activation(transposed(K, c, k)[:, 0:real], tr[b][:, k, 0:real], ACT.Copy,
                                   accum_out=K["node_sums"][:, k, ds(c, 1)]).then_inc(cols_done, 1)
                    if not whole:
                        act.copy(transposed(K, c, k)[:, real:], tr[b][:, k, real:]).then_inc(cols_done, 1)

            if first:
                over_chunks(act, (0, tanh), (1, copy_rows))
            else:
                over_chunks(act, (0, tanh), (2, copy_columns))


def phase_ffn(nc, K, x2_dram, xl_dram, Wr, br, W1, b1, W2, b2, gamma, beta, out):
    with ExitStack() as ctx:
        s = Scope(nc, ctx, "ffn")
        area = K["acc"][:].rearrange("p n k -> p (n k)")
        used = NODES_PAD * DC

        def carve(*shape):
            nonlocal used
            size = 1
            for n in shape:
                size *= n
            part = area[:, used:used + size]
            used += size
            if len(shape) == 2:
                return part.rearrange("p (a b) -> p a b", a=shape[0])
            return part.rearrange("p (a b c) -> p a b c", a=shape[0], b=shape[1])

        U = TOP * HC
        w1 = carve(TOP, DC, HID)
        w2 = carve(TOP, HC, DIM)
        hid = carve(2, U, CHUNK)
        b2_sb = carve(TOP, DIM)
        affine = carve(3, DIM)
        xl = s.sb("xl", [P, 2, 2, DIM])
        x2 = s.sb("x2", [P, 2, 2, DIM])
        y = s.sb("y", [P, 2, 2, DIM])
        o = s.sb("o", [P, 2, 2, DIM])
        mean_b = carve(DC, P)
        b1_sb = s.sb("b1", [P, TOP, HC])
        wr_sb = s.sb("wr", [P, DC, EXPERTS])
        br_sb = s.sb("br", [P, EXPERTS])
        mean = s.sb("mean", [P, DC])
        lg = s.sb("lg", [P, EXPERTS])
        ex = s.sb("ex", [P, EXPERTS])
        rw = s.sb("rw", [P, EXPERTS])
        cap = s.sb("cap", [P, EXPERTS])
        one = s.sb("one", [P, 8])
        top = s.sb("top", [P, 8])
        top_i = s.sb("top_i", [P, 8], U32)
        w_top = s.sb("w_top", [P, TOP])
        stats = s.sb("stats", [P, 2, 2, 6])
        mv = s.sb("mv", [P, 2, 2, 2])
        rstd = s.sb("rstd", [P, 2, 2])
        up = [s.ps(f"up{k}", [P, 512]) for k in range(4)]
        down = [s.ps(f"down{k}", [P, 2, DIM]) for k in range(2)]
        route = s.ps("route", [P, 512])

        small_in = s.sem("small_in")
        routed = s.sem("routed")
        mean_ready = s.sem("mean_ready")
        logits_done = s.sem("logits_done")
        shifted = s.sem("shifted")
        exp_done = s.sem("exp_done")
        top_ready = s.sem("top_ready")
        experts_in = s.sem("experts_in")
        weighted = s.sem("weighted")
        rows_in = [s.sem(f"rows_in{k}") for k in range(2)]
        biased = s.sem("biased")
        up_done = s.sem("up_done")
        gelu_done = s.sem("gelu_done")
        down_done = s.sem("down_done")
        y_done = s.sem("y_done")
        stats_done = s.sem("stats_done")
        mv_done = s.sem("mv_done")
        rstd_half = s.sem("rstd_half")
        rstd_done = s.sem("rstd_done")
        z_done = s.sem("z_done")
        g_done = s.sem("g_done")
        o_done = s.sem("o_done")
        stored = [s.sem(f"stored{k}") for k in range(2)]
        passed = s.sem("passed")
        block = ctx.enter_context(nc.Block())

        @block.sync
        def _(sp):
            sp.dma_start(wr_sb[:], Wr.rearrange("(c p) e -> p c e", p=P)).then_inc(small_in, 16)
            sp.dma_start(br_sb[:], br.partition_broadcast(P)).then_inc(small_in, 16)
            sp.dma_start(affine[:, 0], gamma.partition_broadcast(P)).then_inc(small_in, 16)
            sp.dma_start(affine[:, 1], beta.partition_broadcast(P)).then_inc(small_in, 16)
            sp.wait_ge(top_ready, 1)
            for k in range(TOP):
                e = sp.value_load(top_i[0:1, k:k + 1], min_val=0, max_val=EXPERTS - 1)
                sp.dma_start(w1[:, k], W1[ds(e, 1)].rearrange("o (c p) f -> p (o c) f", p=P)).then_inc(experts_in, 16)
                sp.dma_start(w2[:, k], W2[ds(e, 1)].rearrange("o (c p) d -> p (o c) d", p=P)).then_inc(experts_in, 16)
                sp.dma_start(b1_sb[:, k], b1[ds(e, 1)].rearrange("o (c p) -> p (o c)", p=P),
                             allow_slow_non_contiguous=True).then_inc(experts_in, 16)
                sp.dma_start(b2_sb[:, k], b2[ds(e, 1)].rearrange("o d -> (o d)").partition_broadcast(P)).then_inc(experts_in, 16)

            def load(c, b, n):
                wait_past(sp, o_done, c - 1)
                sp.dma_start(xl[:, b], rows_of(xl_dram, c)).then_inc(rows_in[b], 16)
                sp.dma_start(x2[:, b], rows_of(x2_dram, c)).then_inc(rows_in[b], 16)

            def store(c, b, n):
                sp.wait_ge(o_done, c + 1)
                sp.dma_start(rows_of(out, c), o[:, b]).then_inc(stored[b], 16)

            over_chunks(sp, (0, load), (2, store))
            for k in range(2):
                sp.wait_ge(stored[k], 16 * ((CHUNKS + 1 - k) // 2))

        @block.gpsimd
        def _(pool):
            pool.wait_ge(small_in, 64)
            pool.wait_ge(weighted, 4)

            def add_bias(c, b, n):
                pool.wait_ge(rows_in[b], 32 * (n + 1))
                pool.tensor_tensor(xl[:, b], xl[:, b], affine[:, 2].unsqueeze(1).to_broadcast([P, 2, DIM]),
                                   ALU.add).then_inc(biased, 1)
                pool.tensor_tensor(x2[:, b], x2[:, b], affine[:, 1].unsqueeze(1).to_broadcast([P, 2, DIM]),
                                   ALU.add).then_inc(biased, 1)

            def inverse_deviation(c, b, n):
                pool.wait_ge(mv_done, 2 * c + 2)
                wait_past(pool, z_done, 2 * c - 2)
                pool.tensor_tensor(rstd[:, b], mv[:, b, :, 1], K["eps"][:], ALU.add).then_inc(rstd_half, 1)
                pool.wait_ge(rstd_half, c + 1)
                pool.tensor_tensor(rstd[:, b], rstd[:, b], K["minus_half"][:, 0:2], ALU.pow).then_inc(rstd_done, 1)

            over_chunks(pool, (0, add_bias), (0, inverse_deviation))

        @block.vector
        def _(dve):
            links = 0

            def link(ins):
                nonlocal links
                links += 1
                ins.then_inc(routed, 1)
                dve.wait_ge(routed, links)

            link(dve.tensor_reduce(mean[:], K["node_sums"][:], AX_X, ALU.add))
            link(dve.tensor_scalar(mean[:], mean[:], 1.0 / NODES, None, ALU.mult))
            dve.tensor_copy(mean_b, mean[:].unsqueeze(2).to_broadcast([P, DC, P])).then_inc(mean_ready, 1)
            dve.wait_ge(logits_done, 1)
            dve.wait_ge(small_in, 64)
            link(dve.tensor_tensor(lg[:], route[:, 0:EXPERTS], br_sb[:], ALU.add))

            def softmax(turn):
                link(dve.tensor_reduce(one[:, 0:1], lg[:], AX_X, ALU.max))
                dve.tensor_scalar(lg[:], lg[:], one[:, 0:1], None, ALU.subtract).then_inc(shifted, 1)
                dve.wait_ge(exp_done, turn)
                link(dve.tensor_reduce(one[:, 1:2], ex[:], AX_X, ALU.add))
                link(dve.reciprocal(one[:, 2:3], one[:, 1:2]))
                link(dve.tensor_scalar(rw[:], ex[:], one[:, 2:3], None, ALU.mult))

            softmax(1)
            link(dve.tensor_scalar(cap[:], rw[:], float(NODES), CAPACITY, ALU.mult, ALU.max))
            link(dve.reciprocal(cap[:], cap[:]))
            link(dve.tensor_scalar(cap[:], cap[:], CAPACITY, None, ALU.mult))
            link(dve.tensor_tensor(lg[:], rw[:], cap[:], ALU.mult))
            softmax(2)
            link(dve.max(top[:], rw[:]))
            dve.max_index(top_i[:], top[:], rw[:]).then_inc(top_ready, 1)
            dve.tensor_tensor(lg[:, 0:1], top[:, 1:2], top[:, 0:1], ALU.subtract).then_inc(shifted, 1)
            dve.wait_ge(exp_done, 3)
            link(dve.tensor_scalar(one[:, 3:4], ex[:, 0:1], 1.0, None, ALU.add))
            link(dve.reciprocal(w_top[:, 0:1], one[:, 3:4]))
            link(dve.tensor_tensor(w_top[:, 1:2], ex[:, 0:1], w_top[:, 0:1], ALU.mult))
            dve.wait_ge(experts_in, 128)
            for k in range(TOP):
                dve.tensor_scalar(w2[:, k], w2[:, k], w_top[:, k:k + 1], None, ALU.mult).then_inc(weighted, 1)
            dve.tensor_scalar(affine[:, 2], b2_sb[:, 0], w_top[:, 0:1], None, ALU.mult).then_inc(weighted, 1)
            dve.wait_ge(weighted, 3)
            dve.scalar_tensor_tensor(affine[:, 2], b2_sb[:, 1], w_top[:, 1:2], affine[:, 2], ALU.mult,
                                     ALU.add).then_inc(weighted, 1)

            def moments(c, b, n):
                dve.wait_ge(down_done, c + 1)
                dve.wait_ge(biased, 2 * c + 2)
                dve.tensor_tensor(y[:, b], down[b][:], xl[:, b], ALU.add).then_inc(y_done, 1)
                dve.wait_ge(y_done, c + 1)
                for j in range(2):
                    dve.bn_stats(stats[:, b, j], y[:, b, j]).then_inc(stats_done, 1)
                for j in range(2):
                    wait_apart(dve, stats_done, 2 * c + 1 + j, passed)
                    dve.bn_aggr(mv[:, b, j], stats[:, b, j]).then_inc(mv_done, 1)

            def finish(c, b, n):
                dve.wait_ge(rstd_done, c + 1)
                for j in range(2):
                    dve.tensor_scalar(y[:, b, j], y[:, b, j], mv[:, b, j, 0:1], rstd[:, b, j:j + 1],
                                      ALU.subtract, ALU.mult).then_inc(z_done, 1)
                dve.wait_ge(z_done, 2 * c + 2)
                dve.tensor_tensor(y[:, b], y[:, b], affine[:, 0].unsqueeze(1).to_broadcast([P, 2, DIM]),
                                  ALU.mult).then_inc(g_done, 1)
                dve.wait_ge(g_done, c + 1)
                wait_past(dve, stored[b], 16 * n)
                dve.tensor_tensor(o[:, b], y[:, b], x2[:, b], ALU.add).then_inc(o_done, 1)

            over_chunks(dve, (1, finish), (0, moments))

        @block.tensor
        def _(pe):
            pe.wait_ge(mean_ready, 1)
            pe.wait_ge(small_in, 64)
            for k in range(DC):
                ins = pe.matmul(route[:, 0:EXPERTS], mean_b[:, k], wr_sb[:, k], start=(k == 0), stop=(k == DC - 1))
            ins.then_inc(logits_done, 1)
            pe.wait_ge(experts_in, 128)
            pe.wait_ge(weighted, 2)

            def widen(c, b, n):
                for u in range(U):
                    wait_past(pe, gelu_done, U * c + u - 3)
                    for k in range(DC):
                        ins = pe.matmul(up[u % 4][:, 0:CHUNK], w1[:, u // HC, k, (u % HC) * P:(u % HC + 1) * P],
                                        transposed(K, c, k), start=(k == 0), stop=(k == DC - 1))
                    ins.then_inc(up_done, 1)

            def narrow(c, b, n):
                pe.wait_ge(gelu_done, U * (c + 1))
                wait_past(pe, y_done, c - 1)
                for j in range(2):
                    for u in range(U):
                        ins = pe.matmul(down[b][:, j, :], hid[:, b, u, j * P:(j + 1) * P], w2[:, u // HC, u % HC],
                                        start=(u == 0), stop=(u == U - 1))
                ins.then_inc(down_done, 1)

            over_chunks(pe, (0, widen), (1, narrow))

        @block.scalar
        def _(act):
            for turn in range(2):
                act.wait_ge(shifted, turn + 1)
                act.activation(ex[:], lg[:], ACT.Exp).then_inc(exp_done, 1)
            act.wait_ge(shifted, 3)
            act.activation(ex[:, 0:1], lg[:, 0:1], ACT.Exp).then_inc(exp_done, 1)
            act.wait_ge(experts_in, 128)

            def gelu(c, b, n):
                wait_past(act, down_done, c - 1)
                for u in range(U):
                    act.wait_ge(up_done, U * c + u + 1)
                    act.activation(hid[:, b, u], up[u % 4][:, 0:CHUNK], ACT.Gelu,
                                   bias=b1_sb[:, u // HC, u % HC:u % HC + 1]).then_inc(gelu_done, 1)

            over_chunks(act, (0, gelu))


def build(nc, a, out):
    emb = nc.dram_tensor("emb", [NODES_PAD, DIM], F32, kind="Internal").ap()
    emb_t = nc.dram_tensor("emb_t", [CHUNKS, P, DC * CHUNK], F32, kind="Internal").ap()
    h = nc.dram_tensor("h", [NODES_PAD, DIM], F32, kind="Internal").ap()
    h_t = nc.dram_tensor("h_t", [CHUNKS, P, DC * CHUNK], F32, kind="Internal").ap()
    x2 = nc.dram_tensor("x2", [NODES_PAD, DIM], F32, kind="Internal").ap()
    xl = nc.dram_tensor("xl", [NODES_PAD, DIM], F32, kind="Internal").ap()
    with ExitStack() as ctx:
        K = {}

        def keep(name, shape, dt=F32):
            K[name] = ctx.enter_context(nc.sbuf_tensor(name, shape, dt))

        keep("ident", [P, P])
        keep("ones_r", [P, P], F32R)
        keep("type_of", [P, RCHUNKS])
        keep("minus_type", [P, RCHUNKS])
        keep("minus_half", [P, 2])
        keep("eps", [P, 2])
        keep("zeros", [P, CHUNK, DC])
        keep("node_iota", [P, WIN])
        keep("res", [P, 1])
        keep("node_sums", [P, DC, CHUNKS])
        keep("acc", [P, 2 * ACC_W, DC])
        keep("deg", [P, ACC_W])
        with ExitStack() as edge_tables:
            for name, shape, dt in (("dst", [P, TILES], F32), ("dst_rel", [P, TILES], F32),
                                    ("base", [P, GROUPS], I32), ("acc_at", [P, GROUPS], I32),
                                    ("half_at", [P, GROUPS], I32), ("span", [P, 1], I32)):
                K[name] = edge_tables.enter_context(nc.sbuf_tensor(name, shape, dt))
            phase_setup(nc, K, a["x"], a["dst"], a["L0_gnn_res"], emb, emb_t)
            phase_edges(nc, K, 0, emb, a["L0_gnn_rel1"], a["src"], a["edge_type_400"])
            phase_dense(nc, K, 0, emb_t, h_t, h, a["L0_gnn_W_in1"], a["L0_gnn_W_out1"], a["L0_gnn_W_loop1"],
                        a["L0_gnn_b1"])
            phase_edges(nc, K, 1, h, a["L0_gnn_rel2"], a["src"], a["edge_type_400"])
        phase_dense(nc, K, 1, h_t, None, None, a["L0_gnn_W_in2"], a["L0_gnn_W_out2"], a["L0_gnn_W_loop2"],
                    a["L0_gnn_b2"], (a["x"], a["L0_gnn_mu_w"], a["L0_gnn_mu_b"], x2, xl))
        phase_ffn(nc, K, x2, xl, *(a["L0_ffn_" + n] for n in ("Wr", "br", "W1", "b1", "W2", "b2", "gamma", "beta")),
                  out)


def kernel(**inputs):
    import numpy as np
    from concourse import bacc
    from concourse.bass_utils import run_bass_kernel_spmd

    arrays = {n: np.ascontiguousarray(v) for n, v in inputs.items()}

    def by_tiles(v, fill):
        out = np.full((2, TILES_HALF * P), fill, v.dtype)
        out[:, :HALF] = v.reshape(2, HALF)
        return out.reshape(TILES, P)

    x = np.zeros((NODES_PAD, DIM), arrays["x"].dtype)
    x[:NODES] = arrays["x"]
    arrays["x"] = x
    blocks = by_tiles(arrays["src"], 0).reshape(2 * STEPS, RING // 2, P)
    arrays["src"] = np.ascontiguousarray(blocks.transpose(0, 2, 1))
    arrays["edge_type_400"] = by_tiles(arrays["edge_type_400"], 0).reshape(-1)
    arrays["dst"] = np.ascontiguousarray(by_tiles(arrays["dst"], FAR).T)

    nc = bacc.Bacc("TRN2", target_bir_lowering=False, num_devices=1)
    feeds, args = {}, {}
    for name, v in arrays.items():
        feeds[f"in_{name}"] = v
        args[name] = nc.dram_tensor(f"in_{name}", v.shape, mybir.dt.from_np(v.dtype), kind="ExternalInput").ap()
    out = nc.dram_tensor("out", [NODES_PAD, DIM], F32, kind="ExternalOutput").ap()
    build(nc, args, out)
    r = run_bass_kernel_spmd(nc, [feeds], core_ids=[0])
    return r.results[0]["out"][:NODES]
```

```python
from contextlib import ExitStack

import concourse.bass as bass
from concourse import mybir

ALU = mybir.AluOpType
ACT = mybir.ActivationFunctionType
F32 = mybir.dt.float32
I32 = mybir.dt.int32
U32 = mybir.dt.uint32
F32R = mybir.dt.float32r
AX_X = mybir.AxisListType.X
ds = bass.ds

P = 128
NODES, DIM = 6250, 256
DC = DIM // P
CHUNK = 2 * P
CHUNKS = -(-NODES // CHUNK)
NODES_PAD = CHUNKS * CHUNK
EDGES = 106250
HALF = EDGES // 2
GROUP = 4
RING = 16
GROUPS_IN_RING = RING // GROUP
TILES_HALF = -(-HALF // (P * RING)) * RING
TILES = 2 * TILES_HALF
GROUPS = TILES // GROUP
STEPS = TILES // RING
WIN = 64
HOT_ACT = 2
WINDOWS = -(-NODES // WIN)
ACC_W = NODES_PAD
assert NODES - 1 + WIN <= ACC_W
FAR = 16384
RELS = 400
FULL = RELS // P
REST = RELS - FULL * P
RCHUNKS = FULL + 1
assert 0 < REST and 2 * REST <= P
HID = 512
HC = HID // P
EXPERTS = 8
TOP = 2
EPS = 1e-5
DEEP = 4
BUFS = 4
CAPACITY = float(-(-NODES * 5 // (4 * EXPERTS)))


def wait_past(eng, sem, value):
    if not isinstance(value, int) or value > 0:
        eng.wait_ge(sem, value)


def wait_apart(eng, sem, value, passed):
    if not isinstance(value, int) or value > 0:
        eng.wait_ge(sem, value)
        eng.sem_inc(passed, 1)


def over_chunks(eng, *stages, ring=2, deep=None):
    unroll = deep or ring

    def turn(c, step, q):
        for lag, stage in stages:
            if not isinstance(c, int) or 0 <= c - lag < CHUNKS:
                place = [(q - lag) % ring, unroll // ring * step + (q - lag) // ring]
                if deep:
                    place += [(q - lag) % deep, step + (q - lag) // deep]
                stage(c - lag, *place)

    last = max(lag for lag, _ in stages)
    apart = 2 if deep else 1 - -last // ring
    for c in range(apart * unroll):
        turn(c, c // unroll, c % unroll)
    with eng.Fori(apart, CHUNKS // unroll) as i:
        for q in range(unroll):
            turn(unroll * i + q, i, q)
    for c in range(CHUNKS // unroll * unroll, CHUNKS + last):
        turn(c, c // unroll, c % unroll)


class Scope:

    def __init__(self, nc, ctx, name):
        self.nc, self.ctx, self.name = nc, ctx, name
        self.sems = []
        ctx.callback(self.free)

    def free(self):
        self.nc.clear_and_free_semaphores(self.sems)
        self.nc.all_engine_barrier()

    def sb(self, name, shape, dt=F32):
        return self.ctx.enter_context(self.nc.sbuf_tensor(f"{self.name}_{name}", shape, dt))

    def ps(self, name, shape, dt=F32):
        return self.ctx.enter_context(self.nc.psum_tensor(f"{self.name}_{name}", shape, dt))

    def sem(self, name):
        self.sems.append(self.nc.alloc_semaphore(f"{self.name}_{name}"))
        return self.sems[-1]


def rows_of(dram, c):
    return dram[ds(c * CHUNK, CHUNK), :].rearrange("(j p) d -> p j d", p=P)


def product(pe, out, a, b, first=True, last=True):
    pe.matmul(out, a[1], b[0], start=first, stop=False)
    pe.matmul(out, a[0], b[1], start=False, stop=False)
    return pe.matmul(out, a[0], b[0], start=False, stop=last)


def phase_setup(nc, K, x, dst_tiles, res, emb, emb_t):
    with ExitStack() as ctx:
        s = Scope(nc, ctx, "set")
        dst_i = s.sb("dst_i", [P, TILES], I32)
        neg = s.sb("neg", [P, TILES])
        real = s.sb("real", [P, TILES])
        row_max = s.sb("row_max", [P, 2, GROUPS])
        group_max = s.sb("group_max", [P, 2, GROUPS])
        gmin = group_max[:, 0]
        gmax = group_max[:, 1]
        half_at = s.sb("half_at", [P, GROUPS])
        acc_at = s.sb("acc_at", [P, GROUPS])
        span = s.sb("span", [P, GROUPS])
        span_max = s.sb("span_max", [P, 1])
        x_rows = s.sb("x_rows", [P, BUFS, 2, DIM])
        e_rows = s.sb("e_rows", [P, BUFS, 2, DIM])
        e_t = s.sb("e_t", [P, BUFS, DC, CHUNK])
        stats = s.sb("stats", [P, BUFS, 2, 6])
        mv = s.sb("mv", [P, BUFS, 2, 2])
        rstd = s.sb("rstd", [P, BUFS, 2])
        tr = [s.ps(f"tr{b}", [P, DC, CHUNK]) for b in range(BUFS)]

        dst_in = s.sem("dst_in")
        res_in = s.sem("res_in")
        consts = s.sem("consts")
        zeroed = s.sem("zeroed")
        chain = s.sem("chain")
        reduced = s.sem("reduced")
        x_in = [s.sem(f"x_in{b}") for b in range(BUFS)]
        stats_done = s.sem("stats_done")
        mv_done = s.sem("mv_done")
        rstd_done = s.sem("rstd_done")
        emb_done = s.sem("emb_done")
        tr_done = s.sem("tr_done")
        copied = s.sem("copied")
        stored = [s.sem(f"stored{b}") for b in range(BUFS)]
        passed = s.sem("passed")
        block = ctx.enter_context(nc.Block())

        @block.sync
        def _(sp):
            sp.dma_start(dst_i[:], dst_tiles).then_inc(dst_in, 16)
            sp.dma_start(K["res"][:], res.partition_broadcast(P)).then_inc(res_in, 16)

            def load(c, b, n):
                wait_past(sp, emb_done, c + 1 - BUFS)
                sp.dma_start(x_rows[:, b], rows_of(x, c)).then_inc(x_in[b], 16)

            def store(c, b, n):
                sp.wait_ge(emb_done, c + 1)
                sp.dma_start(rows_of(emb, c), e_rows[:, b]).then_inc(stored[b], 16)
                sp.wait_ge(copied, c + 1)
                sp.dma_start(emb_t[ds(c, 1)].rearrange("o p f -> p (o f)"),
                             e_t[:, b].rearrange("p k n -> p (k n)")).then_inc(stored[b], 16)

            over_chunks(sp, (0, load), (3, store), ring=BUFS)
            sp.wait_ge(res_in, 16)
            for b in range(BUFS):
                sp.wait_ge(stored[b], 32 * -(-(CHUNKS - b) // BUFS))

        @block.gpsimd
        def _(pool):
            pool.memset(K["ident"][:], 0.0).then_inc(consts, 1)
            pool.memset(K["ones_r"][:].bitcast(F32), 1.0).then_inc(consts, 1)
            pool.iota(K["type_of"][:], [[P, RCHUNKS]], base=0, channel_multiplier=1,
                      allow_small_or_imprecise_dtypes=True).then_inc(consts, 1)
            pool.memset(K["minus_half"][:], -0.5).then_inc(consts, 1)
            pool.memset(K["eps"][:], EPS).then_inc(consts, 1)
            pool.memset(K["zeros"][:], 0.0).then_inc(consts, 1)
            pool.iota(K["node_iota"][:], [[1, WIN]], base=0, channel_multiplier=0,
                      allow_small_or_imprecise_dtypes=True).then_inc(consts, 1)
            pool.iota(half_at[:], [[ACC_W, 2], [0, GROUPS // 2]], base=0, channel_multiplier=0,
                      allow_small_or_imprecise_dtypes=True).then_inc(consts, 1)
            pool.wait_ge(consts, 8)
            pool.affine_select(out=K["ident"][:], in_=K["ident"][:], compare_op=ALU.not_equal, fill=1.0,
                               base=0, pattern=[[-1, P]], channel_multiplier=1).then_inc(consts, 1)

            pool.wait_ge(chain, 5)
            pool.partition_all_reduce(group_max[:].rearrange("p h g -> p (h g)"),
                                      row_max[:].rearrange("p h g -> p (h g)"), P,
                                      bass.bass_isa.ReduceOp.max).then_inc(reduced, 1)

            def inverse_deviation(c, b, n):
                pool.wait_ge(mv_done, 2 * c + 2)
                wait_past(pool, emb_done, c + 1 - BUFS)
                pool.tensor_tensor(rstd[:, b], mv[:, b, :, 1], K["eps"][:], ALU.add).then_inc(rstd_done, 1)
                pool.wait_ge(rstd_done, 2 * c + 1)
                pool.tensor_tensor(rstd[:, b], rstd[:, b], K["minus_half"][:, 0:2], ALU.pow).then_inc(rstd_done, 1)

            over_chunks(pool, (0, inverse_deviation), ring=BUFS)

        @block.vector
        def _(dve):
            dve.wait_ge(dst_in, 16)
            dve.tensor_copy(K["dst"][:], dst_i[:]).then_inc(chain, 1)
            dve.wait_ge(chain, 1)
            dve.tensor_scalar(neg[:], K["dst"][:], -1.0, None, ALU.mult).then_inc(chain, 1)
            dve.scalar_tensor_tensor(real[:], K["dst"][:], float(FAR), K["dst"][:],
                                     ALU.is_lt, ALU.mult).then_inc(chain, 1)
            dve.wait_ge(chain, 3)
            for h, v in enumerate((neg, real)):
                dve.tensor_reduce(row_max[:, h], v[:].rearrange("p (g t) -> p g t", t=GROUP), AX_X,
                                  ALU.max).then_inc(chain, 1)

            def moments(c, b, n):
                dve.wait_ge(x_in[b], 16 * (n + 1))
                for j in range(2):
                    dve.bn_stats(stats[:, b, j], x_rows[:, b, j]).then_inc(stats_done, 1)
                wait_past(dve, emb_done, c + 1 - BUFS)
                for j in range(2):
                    wait_apart(dve, stats_done, 2 * c + 1 + j, passed)
                    dve.bn_aggr(mv[:, b, j], stats[:, b, j]).then_inc(mv_done, 1)

            def normalize(c, b, n):
                dve.wait_ge(rstd_done, 2 * c + 2)
                wait_past(dve, stored[b], 32 * n)
                wait_past(dve, tr_done, c + 1 - BUFS)
                for j in range(2):
                    ins = dve.tensor_scalar(e_rows[:, b, j], x_rows[:, b, j], mv[:, b, j, 0:1],
                                            rstd[:, b, j:j + 1], ALU.subtract, ALU.mult)
                ins.then_inc(emb_done, 1)

            over_chunks(dve, (0, moments), (1, normalize), ring=BUFS)

            dve.wait_ge(reduced, 1)
            dve.wait_ge(consts, 9)
            dve.tensor_tensor(span[:], gmax, gmin, ALU.add).then_inc(chain, 1)
            dve.tensor_tensor(K["dst_rel"][:].rearrange("p (g t) -> p g t", t=GROUP),
                              K["dst"][:].rearrange("p (g t) -> p g t", t=GROUP),
                              gmin.unsqueeze(2).to_broadcast([P, GROUPS, GROUP]), ALU.add).then_inc(chain, 1)
            dve.tensor_scalar(K["base"][:], gmin, -1.0, None, ALU.mult).then_inc(chain, 1)
            dve.tensor_tensor(acc_at[:], half_at[:], gmin, ALU.subtract).then_inc(chain, 1)
            dve.tensor_copy(K["half_at"][:], half_at[:]).then_inc(chain, 1)
            dve.wait_ge(chain, 10)
            dve.tensor_copy(K["acc_at"][:], acc_at[:]).then_inc(chain, 1)
            dve.tensor_reduce(span_max[:], span[:], AX_X, ALU.max).then_inc(chain, 1)
            dve.wait_ge(chain, 12)
            dve.tensor_copy(K["span"][:], span_max[:]).then_inc(chain, 1)
            dve.tensor_scalar(K["type_of"][32:64, FULL:], K["type_of"][32:64, FULL:], -32.0, None,
                              ALU.add).then_inc(chain, 1)
            dve.wait_ge(chain, 14)
            dve.tensor_scalar(K["minus_type"][:], K["type_of"][:], -1.0, None, ALU.mult).then_inc(chain, 1)

        @block.tensor
        def _(pe):
            pe.wait_ge(consts, 9)

            def transpose(c, b, n):
                pe.wait_ge(emb_done, c + 1)
                wait_past(pe, copied, c + 1 - BUFS)
                for k in range(DC):
                    for j in range(2):
                        ins = pe.transpose(tr[b][:, k, j * P:(j + 1) * P],
                                           e_rows[:, b, j, k * P:(k + 1) * P], K["ident"][:])
                ins.then_inc(tr_done, 1)

            over_chunks(pe, (0, transpose), ring=BUFS)

        @block.scalar
        def _(act):
            def copy(c, b, n):
                act.wait_ge(tr_done, c + 1)
                wait_past(act, stored[b], 32 * n)
                act.copy(e_t[:, b], tr[b][:]).then_inc(copied, 1)

            def clear(c, b, n):
                for h in range(2):
                    act.copy(K["acc"][:, ds(h * ACC_W + c * CHUNK, CHUNK), :], K["zeros"][:]).then_inc(zeroed, 1)
                act.copy(K["deg"][:, ds(c * CHUNK, CHUNK)], K["zeros"][:, :, 0]).then_inc(zeroed, 1)

            act.wait_ge(consts, 8)
            over_chunks(act, (0, copy), (0, clear), ring=BUFS)


def over_groups(eng, *stages):
    def turn(i, q):
        for lag, stage in stages:
            step = i + (q - lag) // GROUPS_IN_RING
            g = GROUPS_IN_RING * i + q - lag
            if not isinstance(g, int) or 0 <= g < GROUPS:
                stage(g, (q - lag) % GROUPS_IN_RING, step)

    for i in range(2):
        for q in range(GROUPS_IN_RING):
            turn(i, q)
    with eng.Fori(2, STEPS) as i:
        for q in range(GROUPS_IN_RING):
            turn(i, q)
    for t in range(max(lag for lag, _ in stages)):
        turn(STEPS + t // GROUPS_IN_RING, t % GROUPS_IN_RING)


def phase_edges(nc, K, layer, nodes, rel, src_idx, types):
    first = layer == 0
    with ExitStack() as ctx:
        s = Scope(nc, ctx, f"edge{layer}")
        rel_hi = s.sb("rel_hi", [P, RCHUNKS, DIM], F32R)
        rel_lo = s.sb("rel_lo", [P, FULL, DIM], F32R)
        typ = s.sb("typ", [P, 2, GROUP * P], I32)
        hot = s.sb("hot", [P, 2, RCHUNKS, GROUP * P], F32R)
        xg = s.sb("xg", [P, RING, DIM])
        rel_sb = xg[:, RING - RCHUNKS:RING, :]
        m_hi = s.sb("m_hi", [P, 2, GROUP, DIM + 2], F32R)
        m_lo = s.sb("m_lo", [P, 2, GROUP, DIM], F32R)
        sel = s.sb("sel", [P, RING, P], F32R)
        sums_sb = s.sb("sums_sb", [WIN, 2, DIM + 2])
        src_i = s.sb("src_i", [P, 2, RING // 2], I32)
        shifted = s.sb("shifted", [P, GROUP])
        win_base = s.sb("win_base", [P, 1])
        rg = [s.ps(f"rg{b}", [P, GROUP, DIM]) for b in range(2)]
        sums = [s.ps(f"sums{b}", [P, DIM + 2]) for b in range(2)]
        sums_t = [s.ps(f"sums_t{b}", [P, DC + 1, WIN]) for b in range(2)]

        rel_zero = s.sem("rel_zero")
        rel_in = s.sem("rel_in")
        rel_split = s.sem("rel_split")
        src_in = [s.sem(f"src_in{b}") for b in range(2)]
        typ_in = [s.sem(f"typ_in{b}") for b in range(2)]
        gathered = [s.sem(f"gathered{q}") for q in range(GROUPS_IN_RING)]
        hot_done = s.sem("hot_done")
        distances = s.sem("distances")
        hot_act = s.sem("hot_act")
        rel_done = s.sem("rel_done")
        selected = s.sem("selected")
        messages = s.sem("messages")
        hi_done = s.sem("hi_done")
        lo_done = s.sem("lo_done")
        filled = s.sem("filled")
        summed = s.sem("summed")
        sums_copied = s.sem("sums_copied")
        turned = s.sem("turned")
        acc_added = s.sem("acc_added")
        deg_added = s.sem("deg_added")
        win_step = s.sem("win_step")
        win_selected = s.sem("win_selected")
        win_summed = s.sem("win_summed")
        win_added = s.sem("win_added")
        win_deg = s.sem("win_deg")
        passed = s.sem("passed")
        block = ctx.enter_context(nc.Block())

        @block.sync
        def _(sp):
            def load(g, q, i):
                if q % 2 == 0:
                    for k in (q, q + 1):
                        wait_past(sp, gathered[k], 16 * GROUP * i)
                    sp.dma_start(src_i[:, q // 2], src_idx[ds(2 * i + q // 2, 1)].rearrange("o p k -> p (o k)"))\
                      .then_inc(src_in[q // 2], 16)
                wait_past(sp, hot_done, g - 1)
                wait_past(sp, hot_act, g - 1)
                sp.dma_start(typ[:, q % 2], types[ds(g * GROUP * P, GROUP * P)].partition_broadcast(P))\
                  .then_inc(typ_in[q % 2], 16)

            over_groups(sp, (0, load))

        @block.gpsimd
        def _(pool):
            def gather(g, q, i):
                if isinstance(g, int) and g == GROUPS_IN_RING - 1:
                    pool.wait_ge(rel_split, 3)
                wait_apart(pool, lo_done, g + 1 - GROUPS_IN_RING, passed)
                if q % 2 == 0:
                    wait_apart(pool, src_in[q // 2], 16 * (i + 1), passed)
                for t in range(GROUP * q, GROUP * (q + 1)):
                    at = src_i[:, t // (RING // 2), t % (RING // 2):t % (RING // 2) + 1]
                    pool.indirect_dma_start(xg[:, t, :], None, nodes,
                                            bass.IndirectOffsetOnAxis(ap=at, axis=0)).then_inc(gathered[q], 16)

            over_groups(pool, (0, gather))

        @block.scalar
        def _(act):
            act.dma_start(rel_sb[:, 0:FULL, :], rel[0:FULL * P, :].rearrange("(c p) d -> p c d", p=P))\
               .then_inc(rel_in, 16)
            act.wait_ge(rel_zero, 1)
            for at in (0, 32):
                act.dma_start(rel_sb[at:at + REST, FULL, :], rel[FULL * P:RELS, :]).then_inc(rel_in, 16)

            def high(g, q, i):
                act.wait_ge(messages, g + 1)
                wait_past(act, summed, g - 1)
                act.copy(m_hi[:, q % 2, :, 0:DIM], xg[:, GROUP * q:GROUP * (q + 1), :]).then_inc(hi_done, 1)

            def one_hot(g, q, i):
                act.wait_ge(typ_in[q % 2], 16 * ((2 * i + q // 2) + 1))
                wait_past(act, rel_done, g - 1)
                for c in range(HOT_ACT):
                    act.activation(hot[:, q % 2, c], typ[:, q % 2], ACT.Abs,
                                   bias=K["minus_type"][:, c:c + 1]).then_inc(distances, 1)
                for c in range(HOT_ACT):
                    act.wait_ge(distances, HOT_ACT * g + c + 1)
                    ins = act.activation(hot[:, q % 2, c], hot[:, q % 2, c].bitcast(F32), ACT.Relu,
                                         bias=1.0, scale=-1.0)
                ins.then_inc(hot_act, 1)

            def copy_sums(g, q, i):
                act.wait_ge(summed, g + 1)
                wait_past(act, turned, g - 1)
                act.copy(sums_sb[:, q % 2], sums[q % 2][0:WIN, :]).then_inc(sums_copied, 1)

            widest = act.value_load(K["span"][0:1, 0:1], min_val=0, max_val=2 * FAR)
            with act.If(widest < WIN):
                over_groups(act, (4, copy_sums), (0, one_hot), (2, high))
            with act.Else():
                over_groups(act, (0, one_hot), (2, high))

        @block.vector
        def _(dve):
            dve.memset(rel_sb[:, FULL, :], 0.0).then_inc(rel_zero, 1)
            dve.memset(sel[:].bitcast(F32), 0.0).then_inc(filled, 1)
            dve.memset(m_hi[:, :, :, DIM:].bitcast(F32), 0.0).then_inc(filled, 1)
            dve.wait_ge(filled, 2)
            dve.memset(m_hi[:, :, :, DIM:DIM + 1].bitcast(F32), 1.0).then_inc(filled, 1)
            dve.wait_ge(rel_in, 48)
            dve.tensor_copy(rel_hi[:], rel_sb).then_inc(rel_split, 1)
            dve.wait_ge(rel_split, 1)
            dve.tensor_tensor(rel_lo[:], rel_sb[:, 0:FULL, :], rel_hi[:, 0:FULL, :].bitcast(F32),
                              ALU.subtract).then_inc(rel_split, 1)
            dve.tensor_tensor(rel_hi[32:32 + REST, FULL, :], rel_sb[32:32 + REST, FULL, :],
                              rel_hi[32:32 + REST, FULL, :].bitcast(F32), ALU.subtract).then_inc(rel_split, 1)

            def one_hot(g, q, i):
                dve.wait_ge(typ_in[q % 2], 16 * ((2 * i + q // 2) + 1))
                wait_past(dve, rel_done, g - 1)
                for c in range(HOT_ACT, RCHUNKS):
                    ins = dve.tensor_scalar(hot[:, q % 2, c], typ[:, q % 2], K["type_of"][:, c:c + 1], None,
                                            ALU.is_equal)
                ins.then_inc(hot_done, 1)

            def message(g, q, i):
                at = slice(GROUP * q, GROUP * (q + 1))
                dve.wait_ge(gathered[q], 16 * GROUP * (i + 1))
                dve.wait_ge(rel_done, g + 1)
                dve.tensor_tensor(xg[:, at, :], xg[:, at, :], rg[q % 2][:], ALU.mult).then_inc(messages, 1)

            def low(g, q, i):
                dve.wait_ge(hi_done, g + 1)
                wait_past(dve, summed, g - 1)
                dve.tensor_tensor(m_lo[:, q % 2], xg[:, GROUP * q:GROUP * (q + 1), :],
                                  m_hi[:, q % 2, :, 0:DIM].bitcast(F32),
                                  ALU.subtract).then_inc(lo_done, 1)

            def select(out, dst):
                return dve.tensor_tensor(out, K["node_iota"][:].unsqueeze(1).to_broadcast([P, GROUP, WIN]),
                                         dst.unsqueeze(2).to_broadcast([P, GROUP, WIN]), ALU.is_equal)

            def add(b, base, acc_at, added, counted):
                part = K["acc"][:, ds(acc_at, WIN), :]
                dve.tensor_tensor(part, part, sums_t[b][:, 0:DC, :].rearrange("p k n -> p n k"),
                                  ALU.add).then_inc(added, 1)
                if first:
                    part = K["deg"][:, ds(base, WIN)]
                    dve.tensor_tensor(part, part, sums_t[b][:, DC, :], ALU.add).then_inc(counted, 1)

            def short():
                def one_window(g, q, i):
                    wait_past(dve, summed, g + 1 - GROUPS_IN_RING)
                    select(sel[:, GROUP * q:GROUP * (q + 1), 0:WIN],
                           K["dst_rel"][:, ds(GROUP * g, GROUP)]).then_inc(selected, 1)

                def add_window(g, q, i):
                    base = dve.value_load(K["base"][0:1, ds(g, 1)], min_val=0, max_val=ACC_W - WIN) if first else None
                    acc_at = dve.value_load(K["acc_at"][0:1, ds(g, 1)], min_val=0, max_val=2 * ACC_W - WIN)
                    dve.wait_ge(turned, g + 1)
                    wait_past(dve, acc_added, g)
                    if first:
                        wait_past(dve, deg_added, g)
                    add(q % 2, base, acc_at, acc_added, deg_added)

                over_groups(dve, (0, one_hot), (1, one_window), (2, message), (5, add_window), (3, low))

            def long():
                dve.sem_inc(win_added, 1)
                if first:
                    dve.sem_inc(win_deg, 1)

                def all_windows(g, q, i):
                    half_at = dve.value_load(K["half_at"][0:1, ds(g, 1)], min_val=0, max_val=ACC_W)
                    dve.memset(win_base[:], -float(WIN)).then_inc(win_step, 1)
                    with dve.Fori(0, WINDOWS) as w:
                        dve.wait_ge(win_step, g * (2 * WINDOWS + 1) + 2 * w + 1)
                        dve.tensor_scalar(win_base[:], win_base[:], float(WIN), None, ALU.add).then_inc(win_step, 1)
                        dve.wait_ge(win_step, g * (2 * WINDOWS + 1) + 2 * w + 2)
                        dve.tensor_scalar(shifted[:], K["dst"][:, ds(GROUP * g, GROUP)], win_base[:, 0:1], None,
                                          ALU.subtract).then_inc(win_step, 1)
                        dve.wait_ge(win_step, g * (2 * WINDOWS + 1) + 2 * w + 3)
                        select(sel[:, GROUP * q:GROUP * (q + 1), 0:WIN], shifted[:]).then_inc(win_selected, 1)
                        dve.wait_ge(win_summed, g * WINDOWS + w + 1)
                        add(0, w * WIN, half_at + w * WIN, win_added, win_deg)

                over_groups(dve, (0, one_hot), (2, message), (3, low), (3, all_windows))
                dve.wait_ge(win_added, GROUPS * WINDOWS + 1)

            widest = dve.value_load(K["span"][0:1, 0:1], min_val=0, max_val=2 * FAR)
            with dve.If(widest < WIN):
                short()
            with dve.Else():
                long()

        @block.tensor
        def _(pe):
            pe.wait_ge(rel_split, 3)
            pe.wait_ge(filled, 3)

            def relation_rows(g, q, i):
                pe.wait_ge(hot_done, g + 1)
                pe.wait_ge(hot_act, g + 1)
                wait_past(pe, messages, g - 1)
                for t in range(GROUP):
                    for c in range(RCHUNKS):
                        for part in (rel_hi, rel_lo) if c < FULL else (rel_hi,):
                            ins = pe.matmul(rg[q % 2][:, t, :], hot[:, q % 2, c, t * P:(t + 1) * P], part[:, c, :],
                                            start=(c == 0 and part is rel_hi), stop=(c == FULL))
                ins.then_inc(rel_done, 1)

            def short():
                def one_window(g, q, i):
                    pe.wait_ge(selected, g + 1)
                    pe.wait_ge(lo_done, g + 1)
                    wait_past(pe, sums_copied, g - 1)
                    for t in range(GROUP):
                        lhs = sel[:, GROUP * q + t, :]
                        pe.matmul(sums[q % 2][:], lhs, m_hi[:, q % 2, t, :], start=(t == 0), stop=False)
                        ins = pe.matmul(sums[q % 2][:, 0:DIM], lhs, m_lo[:, q % 2, t, :], start=False,
                                        stop=(t == GROUP - 1))
                    ins.then_inc(summed, 1)

                def turn_over(g, q, i):
                    pe.wait_ge(sums_copied, g + 1)
                    if first:
                        wait_past(pe, deg_added, g - 1)
                    wait_apart(pe, acc_added, g - 1, passed)
                    for k in range(DC):
                        ins = pe.transpose(sums_t[q % 2][:, k, :], sums_sb[:, q % 2, k * P:(k + 1) * P],
                                           K["ident"][0:WIN, 0:WIN])
                    if first:
                        ins = pe.transpose(sums_t[q % 2][:, DC, :],
                                           sums_sb[:, q % 2, DIM:DIM + 1].to_broadcast([WIN, P]),
                                           K["ident"][0:WIN, 0:WIN])
                    ins.then_inc(turned, 1)

                over_groups(pe, (1, relation_rows), (3, one_window), (4, turn_over))

            def long():
                def sum_window(q):
                    for k in range(DC):
                        for part in (m_hi, m_lo):
                            for t in range(GROUP):
                                ins = pe.matmul(sums_t[0][:, k, :], part[:, q % 2, t, k * P:(k + 1) * P],
                                                sel[:, GROUP * q + t, 0:WIN], start=(part is m_hi and t == 0),
                                                stop=(part is m_lo and t == GROUP - 1))
                    if first:
                        for t in range(GROUP):
                            ins = pe.matmul(sums_t[0][:, DC, :], K["ones_r"][:], sel[:, GROUP * q + t, 0:WIN],
                                            start=(t == 0), stop=(t == GROUP - 1))
                    return ins

                def all_windows(g, q, i):
                    wait_apart(pe, lo_done, g + 1, passed)
                    with pe.Fori(0, WINDOWS) as w:
                        pe.wait_ge(win_selected, g * WINDOWS + w + 1)
                        pe.wait_ge(win_added, g * WINDOWS + w + 1)
                        if first:
                            pe.wait_ge(win_deg, g * WINDOWS + w + 1)
                        sum_window(q).then_inc(win_summed, 1)
                    pe.wait_ge(win_added, (g + 1) * WINDOWS + 1)
                    pe.sem_inc(summed, 1)

                over_groups(pe, (1, relation_rows), (3, all_windows))

            widest = pe.value_load(K["span"][0:1, 0:1], min_val=0, max_val=2 * FAR)
            with pe.If(widest < WIN):
                short()
            with pe.Else():
                long()


def phase_dense(nc, K, layer, prev_t, next_t, next_rows, W_in, W_out, W_loop, b, tail=None):
    first = layer == 0
    with ExitStack() as ctx:
        s = Scope(nc, ctx, f"dense{layer}")
        n_mat = 3 if first else 4
        work = s.sb("work", [P, 2, 2, DC * CHUNK])
        w_raw = work[:].rearrange("p a b f -> p (a b f)")[:, 0:n_mat * DC * DIM]
        h_t = work[:, 0].rearrange("p b (k n) -> p b k n", k=DC)
        rows = work[:, 1].rearrange("p b (j d) -> p b j d", j=2)
        w = [s.sb(f"w{k}", [P, n_mat, DC, DIM], F32R) for k in range(2)]
        b_sb = s.sb("b", [P, DC])
        prev = s.sb("prev", [P, DEEP, DC, CHUNK])
        prev_parts = [s.sb(f"prev{k}", [P, 2, DC, CHUNK], F32R) for k in range(2)]
        scaled = [s.sb(f"scaled{k}", [P, 2, 2, DC, CHUNK], F32R) for k in range(2)]
        lin = [s.ps(f"lin{k}", [P, DC, CHUNK]) for k in range(2)]
        tr = [s.ps(f"tr{k}", [P, 2, DIM]) for k in range(2)]

        w_in = s.sem("w_in")
        prev_in = [s.sem(f"prev_in{k}") for k in range(DEEP)]
        w_split = s.sem("w_split")
        scaled_done = s.sem("scaled_done")
        scaled_hi = s.sem("scaled_hi")
        scaled_lo = [s.sem(f"scaled_lo{h}") for h in range(2)]
        prev_hi = s.sem("prev_hi")
        prev_lo = s.sem("prev_lo")
        lin_done = s.sem("lin_done")
        tanh_done = s.sem("tanh_done")
        h_done = s.sem("h_done")
        tr_done = s.sem("tr_done")
        rows_done = s.sem("rows_done")
        rows_out = [s.sem(f"rows_out{k}") for k in range(2)]
        if first:
            clamped = s.sem("clamped")
            normed = s.sem("normed")
            cleared = s.sem("cleared")
            t_out = [s.sem(f"t_out{k}") for k in range(2)]
        else:
            x, mu_w, mu_b, x2_dram, xl_dram, Wr, br = tail
            route_in = s.sem("route_in")
            mub_sb = s.sb("mu_b", [P, DIM])
            xb = s.sb("xb", [P, 2, 2, DIM])
            x2 = xb
            h_parts = [s.sb(f"h{k}", [P, DC, CHUNK], F32R) for k in range(2)]
            h_hi = s.sem("h_hi")
            h_lo = s.sem("h_lo")
            stats = s.sb("stats", [P, 2, 2, 6])
            mv = s.sb("mv", [P, 2, 2, 2])
            rstd = s.sb("rstd", [P, 2, 2])
            mu = [s.ps(f"mu{k}", [P, 2, DIM]) for k in range(2)]
            x_in = [s.sem(f"x_in{k}") for k in range(2)]
            xb_done = s.sem("xb_done")
            mu_done = s.sem("mu_done")
            x2_done = s.sem("x2_done")
            stats_done = s.sem("stats_done")
            mv_done = s.sem("mv_done")
            rstd_done = s.sem("rstd_done")
            cols = K["zeros"][:].rearrange("p n k -> p (n k)").rearrange("p (k n) -> p k n", k=DC)
            cols_done = s.sem("cols_done")
            cols_hi = s.sem("cols_hi")
            cols_lo = s.sem("cols_lo")
            x2_out = [s.sem(f"x2_out{k}") for k in range(2)]
        passed = s.sem("passed")
        act_passed = s.sem("act_passed")
        sp_passed = s.sem("sp_passed")

        def sums(h, c):
            return K["acc"][:, ds(h * ACC_W + c * CHUNK, CHUNK), :]

        def degrees(c):
            return K["deg"][:, ds(c * CHUNK, CHUNK)]

        def part(k, c):
            return K["ln_parts"][:, k, ds(c, 1)].rearrange("p o k n -> p (o k) n")

        def copies(c):
            return DC * (c + 1) + (DC if isinstance(c, int) and (c + 1) * CHUNK > NODES else 0)

        block = ctx.enter_context(nc.Block())

        def low_part(eng, h, c, b):
            eng.wait_ge(scaled_hi, 2 * c + h + 1)
            wait_past(eng, lin_done, c - 1)
            eng.tensor_tensor(scaled[1][:, b, h], sums(h, c).rearrange("p n k -> p k n"),
                              scaled[0][:, b, h].bitcast(F32), ALU.subtract).then_inc(scaled_lo[h], 1)

        @block.sync
        def _(sp):
            matrices = (W_in, W_out, W_loop) if first else (W_in, W_out, W_loop, mu_w)
            for k, matrix in enumerate(matrices):
                sp.dma_start(w_raw[:, k * DC * DIM:(k + 1) * DC * DIM].rearrange("p (c m) -> p c m", c=DC),
                             matrix.rearrange("(c p) m -> p c m", p=P)).then_inc(w_in, 16)
            sp.dma_start(b_sb[:], b.rearrange("(c p) -> p c", p=P),
                         allow_slow_non_contiguous=True).then_inc(w_in, 16)
            if not first:
                sp.dma_start(mub_sb[:], mu_b.partition_broadcast(P)).then_inc(w_in, 16)
                sp.dma_start(K["wr"][:], Wr.rearrange("(c p) e -> p c e", p=P)).then_inc(route_in, 16)
                sp.dma_start(K["br"][:], br.partition_broadcast(P)).then_inc(route_in, 16)

            def load(c, b, n, d, m):
                wait_past(sp, h_done, c + 1 - DEEP)
                sp.dma_start(prev[:, d].rearrange("p k n -> p (k n)"),
                             prev_t[ds(c, 1)].rearrange("o p f -> p (o f)")).then_inc(prev_in[d], 16)

            def load_x(c, b, n, d, m):
                wait_apart(sp, rows_done, c - 1, sp_passed)
                wait_past(sp, x2_out[b], 16 * n)
                sp.dma_start(xb[:, b], rows_of(x, c)).then_inc(x_in[b], 16)

            def store_t(c, b, n, d, m):
                sp.wait_ge(h_done, c + 1)
                sp.dma_start(next_t[ds(c, 1)].rearrange("o p f -> p (o f)"),
                             h_t[:, b].rearrange("p k n -> p (k n)")).then_inc(t_out[b], 16)

            def store_rows(c, b, n, d, m):
                sp.wait_ge(rows_done, c + 1)
                sp.dma_start(rows_of(next_rows, c), rows[:, b]).then_inc(rows_out[b], 16)

            def store_x2(c, b, n, d, m):
                sp.wait_ge(x2_done, c + 1)
                sp.dma_start(rows_of(x2_dram, c), x2[:, b]).then_inc(x2_out[b], 16)
                sp.wait_ge(rows_done, c + 1)
                sp.dma_start(rows_of(xl_dram, c), rows[:, b]).then_inc(rows_out[b], 16)

            if first:
                over_chunks(sp, (0, load), (3, store_t), (4, store_rows), deep=DEEP)
            else:
                over_chunks(sp, (0, load), (3, load_x), (4, store_x2), deep=DEEP)
            if not first:
                sp.wait_ge(route_in, 32)
            for k in range(2):
                times = (CHUNKS + 1 - k) // 2
                sp.wait_ge(rows_out[k], 16 * times)
                sp.wait_ge(t_out[k] if first else x2_out[k], 16 * times)

        @block.gpsimd
        def _(pool):
            def previous_low(c, b, n, d, m):
                pool.wait_ge(prev_hi, c + 1)
                wait_past(pool, lin_done, c - 1)
                pool.tensor_tensor(prev_parts[1][:, b], prev[:, d], prev_parts[0][:, b].bitcast(F32),
                                   ALU.subtract).then_inc(prev_lo, 1)

            def scaled_low(c, b, n, d, m):
                low_part(pool, 1, c, b)

            if first:
                over_chunks(pool, (1, scaled_low), (1, previous_low), deep=DEEP)
                return
            pool.wait_ge(w_in, 16 * (n_mat + 2))

            def add_bias(c, b, n, d, m):
                pool.wait_ge(x_in[b], 16 * (n + 1))
                pool.tensor_tensor(xb[:, b], xb[:, b], mub_sb[:].unsqueeze(1).to_broadcast([P, 2, DIM]),
                                   ALU.add).then_inc(xb_done, 1)

            def inverse_deviation(c, b, n, d, m):
                pool.wait_ge(mv_done, 2 * c + 2)
                wait_past(pool, rows_done, c - 1)
                pool.tensor_tensor(rstd[:, b], mv[:, b, :, 1], K["eps"][:], ALU.add).then_inc(rstd_done, 1)
                pool.wait_ge(rstd_done, 2 * c + 1)
                pool.tensor_tensor(rstd[:, b], rstd[:, b], K["minus_half"][:, 0:2], ALU.pow).then_inc(rstd_done, 1)

            def columns_low(c, b, n, d, m):
                pool.wait_ge(cols_done, copies(c))
                pool.wait_ge(cols_hi, c + 1)
                pool.tensor_tensor(part(1, c), cols, part(0, c).bitcast(F32),
                                   ALU.subtract).then_inc(cols_lo, 1)

            def h_low(c, b, n, d, m):
                pool.wait_ge(h_hi, c + 1)
                wait_past(pool, mu_done, c)
                pool.tensor_tensor(h_parts[1][:], h_t[:, b], h_parts[0][:].bitcast(F32), ALU.subtract).then_inc(h_lo, 1)

            over_chunks(pool, (3, h_low), (4, inverse_deviation), (1, previous_low), (3, add_bias),
                        (5, columns_low), deep=DEEP)

        @block.vector
        def _(dve):
            if first:
                dve.tensor_scalar(K["deg"][:], K["deg"][:], 1.0, None, ALU.max).then_inc(clamped, 1)
                dve.wait_ge(clamped, 1)

            def scale(c, b, n, d, m):
                if first:
                    dve.reciprocal(degrees(c), degrees(c)).then_inc(normed, 1)
                    dve.wait_ge(normed, c + 1)
                for h in range(2):
                    dve.tensor_tensor(sums(h, c), sums(h, c), degrees(c).unsqueeze(2).to_broadcast([P, CHUNK, DC]),
                                      ALU.mult).then_inc(scaled_done, 1)

            def scaled_low(c, b, n, d, m):
                low_part(dve, 0, c, b)
                if not first:
                    low_part(dve, 1, c, b)

            def residual(c, b, n, d, m):
                dve.wait_ge(tanh_done, DC * c + DC)
                dve.scalar_tensor_tensor(h_t[:, b], h_t[:, b], K["res"][:, 0:1], prev[:, d], ALU.mult,
                                         ALU.add).then_inc(h_done, 1)

            def moments(c, b, n, d, m):
                dve.wait_ge(mu_done, c + 1)
                dve.wait_ge(xb_done, c + 1)
                dve.tensor_tensor(x2[:, b], xb[:, b], mu[b][:], ALU.add).then_inc(x2_done, 1)
                dve.wait_ge(x2_done, c + 1)
                for j in range(2):
                    dve.bn_stats(stats[:, b, j], x2[:, b, j]).then_inc(stats_done, 1)
                for j in range(2):
                    wait_apart(dve, stats_done, 2 * c + 1 + j, passed)
                    dve.bn_aggr(mv[:, b, j], stats[:, b, j]).then_inc(mv_done, 1)

            def normalize(c, b, n, d, m):
                dve.wait_ge(rstd_done, 2 * c + 2)
                wait_past(dve, tr_done, c - 1)
                wait_past(dve, rows_out[b], 16 * n)
                for j in range(2):
                    ins = dve.tensor_scalar(rows[:, b, j], x2[:, b, j], mv[:, b, j, 0:1], rstd[:, b, j:j + 1],
                                            ALU.subtract, ALU.mult)
                ins.then_inc(rows_done, 1)

            def weights_low(c, *place):
                if isinstance(c, int) and c == 0:
                    dve.wait_ge(w_split, 1)
                    dve.tensor_tensor(w[1][:].rearrange("p a c m -> p (a c m)"), w_raw,
                                      w[0][:].rearrange("p a c m -> p (a c m)").bitcast(F32),
                                      ALU.subtract).then_inc(w_split, 1)

            if first:
                over_chunks(dve, (3, residual), (1, scaled_low), (0, scale), (1, weights_low), deep=DEEP)
            else:
                over_chunks(dve, (3, residual), (4, moments), (1, scaled_low), (4, normalize), (0, scale),
                            (1, weights_low), deep=DEEP)

        @block.tensor
        def _(pe):
            pe.wait_ge(w_split, 2)

            def linear(c, b, n, d, m):
                pe.wait_ge(prev_lo, c + 1)
                for h in range(2):
                    pe.wait_ge(scaled_lo[h], c + 1)
                wait_past(pe, tanh_done, 2 * c - 2)
                for o in range(DC):
                    cols = slice(o * P, (o + 1) * P)
                    for k in range(DC):
                        product(pe, lin[b][:, o, :], [v[:, 2, k, cols] for v in w],
                                [v[:, b, k] for v in prev_parts], k == 0, False)
                    for h in range(2):
                        for k in range(DC):
                            ins = product(pe, lin[b][:, o, :], [v[:, h, k, cols] for v in w],
                                          [v[:, b, h, k] for v in scaled], False, h == 1 and k == DC - 1)
                ins.then_inc(lin_done, 1)

            def to_rows(c, b, n, d, m):
                pe.wait_ge(h_done, c + 1)
                wait_past(pe, rows_done, c - 1)
                for j in range(2):
                    for k in range(DC):
                        ins = pe.transpose(tr[b][:, j, k * P:(k + 1) * P], h_t[:, b, k, j * P:(j + 1) * P],
                                           K["ident"][:])
                ins.then_inc(tr_done, 1)

            def project(c, b, n, d, m):
                pe.wait_ge(h_lo, c + 1)
                wait_past(pe, x2_done, c - 1)
                for j in range(2):
                    for k in range(DC):
                        ins = product(pe, mu[b][:, j, :], [v[:, k, j * P:(j + 1) * P] for v in h_parts],
                                      [v[:, 3, k, :] for v in w], k == 0, k == DC - 1)
                ins.then_inc(mu_done, 1)

            def to_columns(c, b, n, d, m):
                pe.wait_ge(rows_done, c + 1)
                wait_past(pe, cols_hi, c - 1)
                for k in range(DC):
                    for j in range(2):
                        ins = pe.transpose(tr[b][:, k, j * P:(j + 1) * P], rows[:, b, j, k * P:(k + 1) * P],
                                           K["ident"][:])
                ins.then_inc(tr_done, 1)

            if first:
                over_chunks(pe, (0, linear), (1, to_rows), deep=DEEP)
            else:
                over_chunks(pe, (0, linear), (1, project), (2, to_columns), deep=DEEP)

        @block.scalar
        def _(act):
            def first_high(c, *place):
                if isinstance(c, int) and c == 0:
                    scaled_high(c, *place)
                    act.wait_ge(w_in, 16 * (n_mat + (1 if first else 2)))
                    act.copy(w[0][:].rearrange("p a c m -> p (a c m)"), w_raw).then_inc(w_split, 1)

            def previous_high(c, b, n, d, m):
                act.wait_ge(prev_in[d], 16 * (m + 1))
                wait_past(act, lin_done, c - 1)
                act.copy(prev_parts[0][:, b], prev[:, d]).then_inc(prev_hi, 1)

            def scaled_high(c, b, n, d, m):
                for h in range(2):
                    wait_apart(act, scaled_done, 2 * c + h + 1, act_passed)
                    act.copy(scaled[0][:, b, h], sums(h, c).rearrange("p n k -> p k n")).then_inc(scaled_hi, 1)

            def later_high(c, *place):
                if not isinstance(c, int) or c > 0:
                    scaled_high(c, *place)

            def h_high(c, b, n, d, m):
                act.wait_ge(h_done, c + 1)
                wait_past(act, mu_done, c)
                act.copy(h_parts[0][:], h_t[:, b]).then_inc(h_hi, 1)

            def clear(c, b, n, d, m):
                for h in range(2):
                    wait_apart(act, scaled_lo[h], c + 1, act_passed)
                    act.copy(K["acc"][:, ds(h * ACC_W + c * CHUNK, CHUNK), :], K["zeros"][:]).then_inc(cleared, 1)

            def tanh(c, b, n, d, m):
                act.wait_ge(lin_done, c + 1)
                if first:
                    wait_past(act, tr_done, c - 1)
                    wait_past(act, t_out[b], 16 * n)
                else:
                    wait_past(act, h_lo, c - 1)
                for o in range(DC):
                    act.activation(h_t[:, b, o], lin[b][:, o, :], ACT.Tanh, bias=b_sb[:, o:o + 1]).then_inc(tanh_done, 1)

            def copy_rows(c, b, n, d, m):
                act.wait_ge(tr_done, c + 1)
                wait_past(act, rows_out[b], 16 * n)
                act.copy(rows[:, b], tr[b][:]).then_inc(rows_done, 1)

            def copy_columns(c, b, n, d, m):
                act.wait_ge(tr_done, c + 1)
                wait_past(act, cols_lo, c)
                whole = not isinstance(c, int) or (c + 1) * CHUNK <= NODES
                real = CHUNK if whole else NODES - c * CHUNK
                for k in range(DC):
                    act.activation(cols[:, k, 0:real], tr[b][:, k, 0:real], ACT.Copy,
                                   accum_out=K["node_sums"][:, k, ds(c, 1)]).then_inc(cols_done, 1)
                    if not whole:
                        act.copy(cols[:, k, real:], tr[b][:, k, real:]).then_inc(cols_done, 1)
                act.copy(part(0, c), tr[b][:]).then_inc(cols_hi, 1)

            if first:
                over_chunks(act, (3, tanh), (1, first_high), (1, later_high), (1, previous_high), (4, copy_rows),
                            (2, clear), deep=DEEP)
            else:
                over_chunks(act, (3, tanh), (1, first_high), (1, previous_high), (3, h_high), (1, later_high),
                            (5, copy_columns), deep=DEEP)


def phase_ffn(nc, K, x2_dram, xl_dram, W1, b1, W2, b2, gamma, beta, out):
    with ExitStack() as ctx:
        s = Scope(nc, ctx, "ffn")
        U = TOP * HC
        area = K["in_deg"][:]
        used = 0

        def carve(*shape, part):
            nonlocal used
            size = 1
            for n in shape:
                size *= n
            at = part[:, used:used + size]
            used += size
            names = " ".join("abc"[:len(shape)])
            return at.rearrange(f"p ({names}) -> p {names}", **dict(zip("abc", shape[:-1])))

        w1 = [carve(TOP, DC, HID, part=area) for _ in range(2)]
        w2 = [carve(TOP, HC, DIM, part=area), s.sb("w2_lo", [P, TOP, HC, DIM], F32R)[:]]
        mean_b = s.sb("mean_b", [P, DC, P])[:]
        work = s.sb("work", [P, TOP * (HC * DIM + DC * HID)])[:]
        used = 0
        w2_raw = carve(TOP, HC, DIM, part=work)
        w1_raw = carve(TOP, DC, HID, part=work)
        used = 0
        y = carve(2, 2, DIM, part=work)
        o = carve(2, 2, DIM, part=work)
        full = carve(2, U // 2, CHUNK, part=work)
        hid = [s.sb(f"hid{k}", [P, 2, U, CHUNK], F32R) for k in range(2)]
        b2_sb = s.sb("b2", [P, TOP, DIM])
        affine = s.sb("affine", [P, 3, DIM])
        xl = s.sb("xl", [P, 2, 2, DIM])
        x2 = s.sb("x2", [P, 2, 2, DIM])
        b1_sb = s.sb("b1", [P, TOP, HC])
        mean = s.sb("mean", [P, DC])
        lg = s.sb("lg", [P, EXPERTS])
        ex = s.sb("ex", [P, EXPERTS])
        rw = s.sb("rw", [P, EXPERTS])
        cap = s.sb("cap", [P, EXPERTS])
        one = s.sb("one", [P, 8])
        top = s.sb("top", [P, 8])
        top_i = s.sb("top_i", [P, 8], U32)
        w_top = s.sb("w_top", [P, TOP])
        stats = s.sb("stats", [P, 2, 2, 6])
        mv = s.sb("mv", [P, 2, 2, 2])
        rstd = s.sb("rstd", [P, 2, 2])
        up = [s.ps(f"up{k}", [P, 512]) for k in range(4)]
        down = [s.ps(f"down{k}", [P, 2, DIM]) for k in range(2)]
        route = s.ps("route", [P, 512])

        small_in = s.sem("small_in")
        routed = s.sem("routed")
        mean_ready = s.sem("mean_ready")
        logits_done = s.sem("logits_done")
        shifted = s.sem("shifted")
        exp_done = s.sem("exp_done")
        top_ready = s.sem("top_ready")
        w1_in = [s.sem(f"w1_in{k}") for k in range(TOP)]
        b1_in = s.sem("b1_in")
        w1_hi = s.sem("w1_hi")
        w1_lo = s.sem("w1_lo")
        w2_split = s.sem("w2_split")
        experts_in = s.sem("experts_in")
        weighted = s.sem("weighted")
        rows_in = [s.sem(f"rows_in{k}") for k in range(2)]
        biased = s.sem("biased")
        up_done = s.sem("up_done")
        gelu_done = s.sem("gelu_done")
        hid_hi = s.sem("hid_hi")
        hid_lo = s.sem("hid_lo")
        down_done = s.sem("down_done")
        y_done = s.sem("y_done")
        stats_done = s.sem("stats_done")
        mv_done = s.sem("mv_done")
        rstd_done = s.sem("rstd_done")
        z_done = s.sem("z_done")
        g_done = s.sem("g_done")
        o_done = s.sem("o_done")
        stored = [s.sem(f"stored{k}") for k in range(2)]
        passed = s.sem("passed")
        block = ctx.enter_context(nc.Block())

        @block.sync
        def _(sp):
            sp.dma_start(affine[:, 0], gamma.partition_broadcast(P)).then_inc(small_in, 16)
            sp.dma_start(affine[:, 1], beta.partition_broadcast(P)).then_inc(small_in, 16)
            sp.wait_ge(top_ready, 1)
            chosen = [sp.value_load(top_i[0:1, k:k + 1], min_val=0, max_val=EXPERTS - 1) for k in range(TOP)]
            for k, e in enumerate(chosen):
                sp.dma_start(w1_raw[:, k], W1[ds(e, 1)].rearrange("o (c p) f -> p (o c) f", p=P)).then_inc(w1_in[k], 16)
                sp.dma_start(b1_sb[:, k], b1[ds(e, 1)].rearrange("o (c p) -> p (o c)", p=P),
                             allow_slow_non_contiguous=True).then_inc(b1_in, 16)
            for k, e in enumerate(chosen):
                sp.dma_start(w2_raw[:, k], W2[ds(e, 1)].rearrange("o (c p) d -> p (o c) d", p=P)).then_inc(experts_in, 16)
                sp.dma_start(b2_sb[:, k], b2[ds(e, 1)].rearrange("o d -> (o d)").partition_broadcast(P)).then_inc(experts_in, 16)

            def load(c, b, n):
                wait_past(sp, o_done, c - 1)
                sp.dma_start(xl[:, b], rows_of(xl_dram, c)).then_inc(rows_in[b], 16)
                sp.dma_start(x2[:, b], rows_of(x2_dram, c)).then_inc(rows_in[b], 16)

            def store(c, b, n):
                sp.wait_ge(o_done, c + 1)
                sp.dma_start(rows_of(out, c), o[:, b]).then_inc(stored[b], 16)

            over_chunks(sp, (0, load), (2, store))
            for k in range(2):
                sp.wait_ge(stored[k], 16 * ((CHUNKS + 1 - k) // 2))

        @block.gpsimd
        def _(pool):
            pool.wait_ge(small_in, 32)
            pool.wait_ge(weighted, 4)

            def add_bias(c, b, n):
                pool.wait_ge(rows_in[b], 32 * (n + 1))
                pool.tensor_tensor(xl[:, b], xl[:, b], affine[:, 2].unsqueeze(1).to_broadcast([P, 2, DIM]),
                                   ALU.add).then_inc(biased, 1)
                pool.tensor_tensor(x2[:, b], x2[:, b], affine[:, 1].unsqueeze(1).to_broadcast([P, 2, DIM]),
                                   ALU.add).then_inc(biased, 1)

            def inverse_deviation(c, b, n):
                pool.wait_ge(mv_done, 2 * c + 2)
                wait_past(pool, z_done, 2 * c - 2)
                pool.tensor_tensor(rstd[:, b], mv[:, b, :, 1], K["eps"][:], ALU.add).then_inc(rstd_done, 1)
                pool.wait_ge(rstd_done, 2 * c + 1)
                pool.tensor_tensor(rstd[:, b], rstd[:, b], K["minus_half"][:, 0:2], ALU.pow).then_inc(rstd_done, 1)

            over_chunks(pool, (0, add_bias), (0, inverse_deviation))

        @block.vector
        def _(dve):
            links = 0

            def link(ins):
                nonlocal links
                links += 1
                ins.then_inc(routed, 1)
                dve.wait_ge(routed, links)

            link(dve.tensor_reduce(mean[:], K["node_sums"][:], AX_X, ALU.add))
            link(dve.tensor_scalar(mean[:], mean[:], 1.0 / NODES, None, ALU.mult))
            dve.tensor_copy(mean_b, mean[:].unsqueeze(2).to_broadcast([P, DC, P])).then_inc(mean_ready, 1)
            dve.wait_ge(logits_done, 1)
            link(dve.tensor_tensor(lg[:], route[:, 0:EXPERTS], K["br"][:], ALU.add))

            def softmax(turn):
                link(dve.tensor_reduce(one[:, 0:1], lg[:], AX_X, ALU.max))
                dve.tensor_scalar(lg[:], lg[:], one[:, 0:1], None, ALU.subtract).then_inc(shifted, 1)
                dve.wait_ge(exp_done, turn)
                link(dve.tensor_reduce(one[:, 1:2], ex[:], AX_X, ALU.add))
                link(dve.reciprocal(one[:, 2:3], one[:, 1:2]))
                link(dve.tensor_scalar(rw[:], ex[:], one[:, 2:3], None, ALU.mult))

            softmax(1)
            link(dve.tensor_scalar(cap[:], rw[:], float(NODES), CAPACITY, ALU.mult, ALU.max))
            link(dve.reciprocal(cap[:], cap[:]))
            link(dve.tensor_scalar(cap[:], cap[:], CAPACITY, None, ALU.mult))
            link(dve.tensor_tensor(lg[:], rw[:], cap[:], ALU.mult))
            softmax(2)
            link(dve.max(top[:], rw[:]))
            dve.max_index(top_i[:], top[:], rw[:]).then_inc(top_ready, 1)
            dve.tensor_tensor(lg[:, 0:1], top[:, 1:2], top[:, 0:1], ALU.subtract).then_inc(shifted, 1)
            dve.wait_ge(exp_done, 3)
            link(dve.tensor_scalar(one[:, 3:4], ex[:, 0:1], 1.0, None, ALU.add))
            link(dve.reciprocal(w_top[:, 0:1], one[:, 3:4]))
            link(dve.tensor_tensor(w_top[:, 1:2], ex[:, 0:1], w_top[:, 0:1], ALU.mult))
            for k in range(TOP):
                dve.wait_ge(w1_hi, k + 1)
                dve.tensor_tensor(w1[1][:, k], w1_raw[:, k], w1[0][:, k].bitcast(F32), ALU.subtract).then_inc(w1_lo, 1)
            dve.wait_ge(experts_in, 64)
            for k in range(TOP):
                dve.tensor_scalar(w2_raw[:, k], w2_raw[:, k], w_top[:, k:k + 1], None, ALU.mult).then_inc(weighted, 1)
            dve.tensor_scalar(affine[:, 2], b2_sb[:, 0], w_top[:, 0:1], None, ALU.mult).then_inc(weighted, 1)
            dve.wait_ge(weighted, 3)
            dve.scalar_tensor_tensor(affine[:, 2], b2_sb[:, 1], w_top[:, 1:2], affine[:, 2], ALU.mult,
                                     ALU.add).then_inc(weighted, 1)

            def w2_low(c, *place):
                if isinstance(c, int) and c == 0:
                    dve.wait_ge(w2_split, 1)
                    dve.tensor_tensor(w2[1], w2_raw, w2[0].bitcast(F32), ALU.subtract).then_inc(w2_split, 1)

            def low(half):
                def stage(c, b, n):
                    dve.wait_ge(hid_hi, 2 * c + half + 1)
                    at = slice(half * U // 2, (half + 1) * U // 2)
                    dve.tensor_tensor(hid[1][:, b, at], full[:, half], hid[0][:, b, at].bitcast(F32),
                                      ALU.subtract).then_inc(hid_lo, 1)
                return stage

            def moments(c, b, n):
                dve.wait_ge(down_done, c + 1)
                dve.wait_ge(biased, 2 * c + 2)
                dve.tensor_tensor(y[:, b], down[b][:], xl[:, b], ALU.add).then_inc(y_done, 1)
                dve.wait_ge(y_done, c + 1)
                for j in range(2):
                    dve.bn_stats(stats[:, b, j], y[:, b, j]).then_inc(stats_done, 1)
                for j in range(2):
                    wait_apart(dve, stats_done, 2 * c + 1 + j, passed)
                    dve.bn_aggr(mv[:, b, j], stats[:, b, j]).then_inc(mv_done, 1)

            def finish(c, b, n):
                dve.wait_ge(rstd_done, 2 * c + 2)
                for j in range(2):
                    dve.tensor_scalar(y[:, b, j], y[:, b, j], mv[:, b, j, 0:1], rstd[:, b, j:j + 1],
                                      ALU.subtract, ALU.mult).then_inc(z_done, 1)
                dve.wait_ge(z_done, 2 * c + 2)
                dve.tensor_tensor(y[:, b], y[:, b], affine[:, 0].unsqueeze(1).to_broadcast([P, 2, DIM]),
                                  ALU.mult).then_inc(g_done, 1)
                dve.wait_ge(g_done, c + 1)
                wait_past(dve, stored[b], 16 * n)
                dve.tensor_tensor(o[:, b], y[:, b], x2[:, b], ALU.add).then_inc(o_done, 1)

            over_chunks(dve, (2, moments), (0, low(0)), (2, finish), (0, low(1)), (0, w2_low))

        @block.tensor
        def _(pe):
            pe.wait_ge(mean_ready, 1)
            for k in range(DC):
                ins = pe.matmul(route[:, 0:EXPERTS], mean_b[:, k], K["wr"][:, k], start=(k == 0), stop=(k == DC - 1))
            ins.then_inc(logits_done, 1)

            def widen(c, b, n):
                for u in range(U):
                    if isinstance(c, int) and c == 0 and u % HC == 0:
                        pe.wait_ge(w1_lo, u // HC + 1)
                    wait_past(pe, gelu_done, U * c + u - 3)
                    for k in range(DC):
                        ins = product(pe, up[u % 4][:, 0:CHUNK],
                                      [w[:, u // HC, k, (u % HC) * P:(u % HC + 1) * P] for w in w1],
                                      [K["ln_parts"][:, part, ds(c, 1), k].rearrange("p o n -> p (o n)") for part in range(2)],
                                      k == 0, k == DC - 1)
                    ins.then_inc(up_done, 1)

            def narrow(c, b, n):
                pe.wait_ge(hid_lo, 2 * c + 2)
                wait_past(pe, y_done, c - 1)
                if isinstance(c, int) and c == 0:
                    pe.wait_ge(w2_split, 2)
                for j in range(2):
                    for u in range(U):
                        ins = product(pe, down[b][:, j, :], [h[:, b, u, j * P:(j + 1) * P] for h in hid],
                                      [w[:, u // HC, u % HC] for w in w2],
                                      u == 0, u == U - 1)
                ins.then_inc(down_done, 1)

            over_chunks(pe, (0, widen), (1, narrow))

        @block.scalar
        def _(act):
            for turn in range(2):
                act.wait_ge(shifted, turn + 1)
                act.activation(ex[:], lg[:], ACT.Exp).then_inc(exp_done, 1)
            act.wait_ge(shifted, 3)
            act.activation(ex[:, 0:1], lg[:, 0:1], ACT.Exp).then_inc(exp_done, 1)
            for k in range(TOP):
                act.wait_ge(w1_in[k], 16)
                act.copy(w1[0][:, k], w1_raw[:, k]).then_inc(w1_hi, 1)
            act.wait_ge(b1_in, 16 * TOP)

            def w2_high(c, *place):
                if isinstance(c, int) and c == 0:
                    act.wait_ge(weighted, 2)
                    act.copy(w2[0], w2_raw).then_inc(w2_split, 1)

            def gelu(half):
                def stage(c, b, n):
                    wait_past(act, hid_lo, 2 * c + half - 1)
                    for v in range(U // 2):
                        u = half * U // 2 + v
                        act.wait_ge(up_done, U * c + u + 1)
                        act.activation(full[:, half, v], up[u % 4][:, 0:CHUNK], ACT.Gelu,
                                       bias=b1_sb[:, u // HC, u % HC:u % HC + 1]).then_inc(gelu_done, 1)
                return stage

            def high(half):
                def stage(c, b, n):
                    act.wait_ge(gelu_done, U * c + (half + 1) * U // 2)
                    wait_past(act, down_done, c - 1)
                    act.copy(hid[0][:, b, half * U // 2:(half + 1) * U // 2], full[:, half]).then_inc(hid_hi, 1)
                return stage

            over_chunks(act, (0, gelu(0)), (0, high(0)), (0, gelu(1)), (0, high(1)), (0, w2_high))


def build(nc, a, out):
    emb = nc.dram_tensor("emb", [NODES_PAD, DIM], F32, kind="Internal").ap()
    emb_t = nc.dram_tensor("emb_t", [CHUNKS, P, DC * CHUNK], F32, kind="Internal").ap()
    h = nc.dram_tensor("h", [NODES_PAD, DIM], F32, kind="Internal").ap()
    h_t = nc.dram_tensor("h_t", [CHUNKS, P, DC * CHUNK], F32, kind="Internal").ap()
    x2 = nc.dram_tensor("x2", [NODES_PAD, DIM], F32, kind="Internal").ap()
    xl = nc.dram_tensor("xl", [NODES_PAD, DIM], F32, kind="Internal").ap()
    with ExitStack() as ctx:
        K = {}

        def keep(name, shape, dt=F32):
            K[name] = ctx.enter_context(nc.sbuf_tensor(name, shape, dt))

        for name, shape, alias, alias_shape in (("acc", [P, 2 * ACC_W, DC], "ln_parts", [P, 2, CHUNKS, DC, CHUNK]),
                                                ("deg", [P, ACC_W], "in_deg", [P, ACC_W])):
            at = -(-nc.sbuf_base // 32) * 32
            keep(name, shape)
            K[alias] = nc.alloc_sbuf_tensor_at(alias, alias_shape, F32R, offset=at)
            assert nc.sbuf_base == at + 4 * shape[1] * (shape[2] if len(shape) == 3 else 1)
        keep("ident", [P, P])
        keep("ones_r", [P, P], F32R)
        keep("type_of", [P, RCHUNKS])
        keep("minus_type", [P, RCHUNKS])
        keep("minus_half", [P, 2])
        keep("eps", [P, 2])
        keep("zeros", [P, CHUNK, DC])
        keep("node_iota", [P, WIN])
        keep("res", [P, 1])
        keep("node_sums", [P, DC, CHUNKS])
        with ExitStack() as edge_tables:
            for name, shape, dt in (("dst", [P, TILES], F32), ("dst_rel", [P, TILES], F32),
                                    ("base", [P, GROUPS], I32), ("acc_at", [P, GROUPS], I32),
                                    ("half_at", [P, GROUPS], I32), ("span", [P, 1], I32)):
                K[name] = edge_tables.enter_context(nc.sbuf_tensor(name, shape, dt))
            phase_setup(nc, K, a["x"], a["dst"], a["L0_gnn_res"], emb, emb_t)
            phase_edges(nc, K, 0, emb, a["L0_gnn_rel1"], a["src"], a["edge_type_400"])
            phase_dense(nc, K, 0, emb_t, h_t, h, a["L0_gnn_W_in1"], a["L0_gnn_W_out1"], a["L0_gnn_W_loop1"],
                        a["L0_gnn_b1"])
            phase_edges(nc, K, 1, h, a["L0_gnn_rel2"], a["src"], a["edge_type_400"])
        keep("wr", [P, DC, EXPERTS])
        keep("br", [P, EXPERTS])
        phase_dense(nc, K, 1, h_t, None, None, a["L0_gnn_W_in2"], a["L0_gnn_W_out2"], a["L0_gnn_W_loop2"],
                    a["L0_gnn_b2"], (a["x"], a["L0_gnn_mu_w"], a["L0_gnn_mu_b"], x2, xl, a["L0_ffn_Wr"],
                                          a["L0_ffn_br"]))
        phase_ffn(nc, K, x2, xl, *(a["L0_ffn_" + n] for n in ("W1", "b1", "W2", "b2", "gamma", "beta")),
                  out)


def kernel(**inputs):
    import numpy as np
    from concourse import bacc
    from concourse.bass_utils import run_bass_kernel_spmd

    arrays = {n: np.ascontiguousarray(v) for n, v in inputs.items()}

    def by_tiles(v, fill):
        out = np.full((2, TILES_HALF * P), fill, v.dtype)
        out[:, :HALF] = v.reshape(2, HALF)
        return out.reshape(TILES, P)

    x = np.zeros((NODES_PAD, DIM), arrays["x"].dtype)
    x[:NODES] = arrays["x"]
    arrays["x"] = x
    blocks = by_tiles(arrays["src"], 0).reshape(2 * STEPS, RING // 2, P)
    arrays["src"] = np.ascontiguousarray(blocks.transpose(0, 2, 1))
    arrays["edge_type_400"] = by_tiles(arrays["edge_type_400"], 0).reshape(-1)
    arrays["dst"] = np.ascontiguousarray(by_tiles(arrays["dst"], FAR).T)

    nc = bacc.Bacc("TRN2", target_bir_lowering=False, num_devices=1)
    feeds, args = {}, {}
    for name, v in arrays.items():
        feeds[f"in_{name}"] = v
        args[name] = nc.dram_tensor(f"in_{name}", v.shape, mybir.dt.from_np(v.dtype), kind="ExternalInput").ap()
    out = nc.dram_tensor("out", [NODES_PAD, DIM], F32, kind="ExternalOutput").ap()
    build(nc, args, out)
    r = run_bass_kernel_spmd(nc, [feeds], core_ids=[0])
    return r.results[0]["out"][:NODES]
```
